# Optimizing a Trainium2 kernel written in Bass

```python
import numpy as np
import jax
import jax.numpy as jnp

def _softmax(x, axis=-1):
    return jax.nn.softmax(x, axis=axis)

def _gelu(x):
    return jax.nn.gelu(x, approximate=True)

def _silu(x):
    return jax.nn.silu(x)

def _sigmoid(x):
    return jax.nn.sigmoid(x)

def _layernorm(x, axis=-1, eps=1e-05):
    m = jnp.mean(x, axis=axis, keepdims=True)
    v = jnp.var(x, axis=axis, keepdims=True)
    return (x - m) / jnp.sqrt(v + eps)

def _scatter_add(tgt, idx, src, axis=0):
    return tgt.at[idx].add(src)

def _segment_sum(src, seg, n):
    return jax.ops.segment_sum(src, seg, n)
kernel_name = 'mk_gnn_ffn_d1_gnn_r8_fc57de'

def setup_inputs(seed: int=0):
    np.random.seed(seed)
    _w = jnp.asarray

    def _rec_inputs():
        import jax
        import jax.numpy as jnp
        _gk = jax.random.key(seed)
        x = -0.0005963 + 1.001 * jax.random.normal(jax.random.fold_in(_gk, 1), (384, 1024), jnp.float32)
        _s = jax.random.randint(jax.random.fold_in(_gk, 2), (3072,), 0, 384, jnp.int32)
        _d = jax.random.randint(jax.random.fold_in(_gk, 3), (3072,), 0, 384, jnp.int32)
        _loop = jnp.arange(384, dtype=jnp.int32)
        src = jnp.concatenate([_s, _d, _loop])
        dst = jnp.concatenate([_d, _s, _loop])
        _o = jnp.argsort(dst, stable=True)
        src = src[_o]
        dst = dst[_o]
        edge_type_5 = jax.random.randint(jax.random.fold_in(_gk, 12), (6528,), 0, 5, jnp.int32)
        return (x, src, dst, edge_type_5)
    x, src, dst, edge_type_5 = _rec_inputs()

    def _L0_gnn_setup():
        import jax, jax.numpy as jnp
        import numpy as np
        N = 384
        E = 12288
        IN_F = 1024
        OUT_F = 1024
        H = 16
        D = OUT_F // H
        NUM_ETYPES = 4

        def _build_mask(edge_index, edge_type, edge_type_weights, dtype):
            src, dst = (edge_index[0], edge_index[1])
            w = jax.nn.softplus(edge_type_weights)
            mask = jnp.full((N, N), -jnp.inf, dtype=dtype)
            mask = mask.at[src, dst].set(w[edge_type - 1])
            diag = jnp.diagonal(mask)
            idx = jnp.arange(N)
            mask = mask.at[idx, idx].set(jnp.where(jnp.isneginf(diag), w[3], diag))
            return mask
        key = jax.random.key(seed)
        ks = jax.random.split(key, 20)
        p = lambda k, shape: jax.random.normal(k, shape, dtype=jnp.float32) * 0.02
        return {'x': jax.random.normal(ks[0], (N, IN_F), dtype=jnp.float32), 'edge_index': jax.random.randint(ks[1], (2, E), 0, N), 'edge_type': jax.random.randint(ks[2], (E,), 1, NUM_ETYPES + 1), 'edge_type_weights': jnp.ones((NUM_ETYPES,), jnp.float32) + 0.1 * jax.random.normal(ks[3], (NUM_ETYPES,), dtype=jnp.float32), 'wq': p(ks[4], (OUT_F, IN_F)), 'bq': p(ks[5], (OUT_F,)), 'wk': p(ks[6], (OUT_F, IN_F)), 'bk': p(ks[7], (OUT_F,)), 'wv': p(ks[8], (OUT_F, IN_F)), 'bv': p(ks[9], (OUT_F,)), 'wiq': p(ks[10], (OUT_F, OUT_F)), 'biq': p(ks[11], (OUT_F,)), 'wik': p(ks[12], (OUT_F, OUT_F)), 'bik': p(ks[13], (OUT_F,)), 'wiv': p(ks[14], (OUT_F, OUT_F)), 'biv': p(ks[15], (OUT_F,)), 'wo': p(ks[16], (OUT_F, OUT_F)), 'bo': p(ks[17], (OUT_F,))}
    _L0_gnn_all = _L0_gnn_setup()
    _L0_gnn_in = {k: v for k, v in _L0_gnn_all.items() if k in ('edge_type_weights', 'wq', 'bq', 'wk', 'bk', 'wv', 'bv', 'wiq', 'biq', 'wik', 'bik', 'wiv', 'biv', 'wo', 'bo')}
    del _L0_gnn_all

    def _L0_ffn_setup():
        import jax, jax.numpy as jnp
        import numpy as np
        QMAX = 127.0

        def _ste_round(v):
            return v + jax.lax.stop_gradient(jnp.round(v) - v)

        def _act_fake_quant(x, clip_factor):
            scale = jax.nn.sigmoid(clip_factor) * jnp.max(jnp.abs(x)) / QMAX
            return jnp.clip(_ste_round(x / scale), -QMAX - 1.0, QMAX) * scale

        def _weight_fake_quant(w):
            scale = jnp.max(jnp.abs(w), axis=1, keepdims=True) / QMAX
            return jnp.clip(_ste_round(w / scale), -QMAX - 1.0, QMAX) * scale
        key = jax.random.key(seed)
        k1, k2, k3, k4 = jax.random.split(key, 4)
        B, S, H, I = (8, 1024, 1024, 352)
        return {'x': jax.random.normal(k1, (B, S, H), dtype=jnp.float32), 'clip_x': jnp.full((1,), 4.0, dtype=jnp.float32), 'clip_down': jnp.full((1,), 4.0, dtype=jnp.float32), 'w_gate': jax.random.normal(k2, (I, H), dtype=jnp.float32) * 0.02, 'w_up': jax.random.normal(k3, (I, H), dtype=jnp.float32) * 0.02, 'w_down': jax.random.normal(k4, (H, I), dtype=jnp.float32) * 0.02}
    _L0_ffn_all = _L0_ffn_setup()
    _L0_ffn_in = {k: v for k, v in _L0_ffn_all.items() if k in ('clip_x', 'clip_down', 'w_gate', 'w_up', 'w_down')}
    del _L0_ffn_all
    return {'x': x, 'src': src, 'dst': dst, 'edge_type_5': edge_type_5, 'L0_gnn_edge_type_weights': _L0_gnn_in['edge_type_weights'], 'L0_gnn_wq': _L0_gnn_in['wq'], 'L0_gnn_bq': _L0_gnn_in['bq'], 'L0_gnn_wk': _L0_gnn_in['wk'], 'L0_gnn_bk': _L0_gnn_in['bk'], 'L0_gnn_wv': _L0_gnn_in['wv'], 'L0_gnn_bv': _L0_gnn_in['bv'], 'L0_gnn_wiq': _L0_gnn_in['wiq'], 'L0_gnn_biq': _L0_gnn_in['biq'], 'L0_gnn_wik': _L0_gnn_in['wik'], 'L0_gnn_bik': _L0_gnn_in['bik'], 'L0_gnn_wiv': _L0_gnn_in['wiv'], 'L0_gnn_biv': _L0_gnn_in['biv'], 'L0_gnn_wo': _L0_gnn_in['wo'], 'L0_gnn_bo': _L0_gnn_in['bo'], 'L0_ffn_clip_x': _L0_ffn_in['clip_x'], 'L0_ffn_clip_down': _L0_ffn_in['clip_down'], 'L0_ffn_w_gate': _L0_ffn_in['w_gate'], 'L0_ffn_w_up': _L0_ffn_in['w_up'], 'L0_ffn_w_down': _L0_ffn_in['w_down']}

def reference(x, src, dst, edge_type_5, L0_gnn_edge_type_weights, L0_gnn_wq, L0_gnn_bq, L0_gnn_wk, L0_gnn_bk, L0_gnn_wv, L0_gnn_bv, L0_gnn_wiq, L0_gnn_biq, L0_gnn_wik, L0_gnn_bik, L0_gnn_wiv, L0_gnn_biv, L0_gnn_wo, L0_gnn_bo, L0_ffn_clip_x, L0_ffn_clip_down, L0_ffn_w_gate, L0_ffn_w_up, L0_ffn_w_down):
    import jax
    import jax.numpy as jnp

    def _L0_gnn_ref(x, edge_index, edge_type, edge_type_weights, wq, bq, wk, bk, wv, bv, wiq, biq, wik, bik, wiv, biv, wo, bo):
        import jax, jax.numpy as jnp
        import numpy as np
        N = 384
        E = 12288
        IN_F = 1024
        OUT_F = 1024
        H = 16
        D = OUT_F // H
        NUM_ETYPES = 4

        def _build_mask(edge_index, edge_type, edge_type_weights, dtype):
            src, dst = (edge_index[0], edge_index[1])
            w = jax.nn.softplus(edge_type_weights)
            mask = jnp.full((N, N), -jnp.inf, dtype=dtype)
            mask = mask.at[src, dst].set(w[edge_type - 1])
            diag = jnp.diagonal(mask)
            idx = jnp.arange(N)
            mask = mask.at[idx, idx].set(jnp.where(jnp.isneginf(diag), w[3], diag))
            return mask
        q = x @ wq.T + bq
        k = x @ wk.T + bk
        v = x @ wv.T + bv
        q2 = (q @ wiq.T + biq).reshape(N, H, D).transpose(1, 0, 2)
        k2 = (k @ wik.T + bik).reshape(N, H, D).transpose(1, 0, 2)
        v2 = (v @ wiv.T + biv).reshape(N, H, D).transpose(1, 0, 2)
        mask = _build_mask(edge_index, edge_type, edge_type_weights, x.dtype)
        scale = 1.0 / np.sqrt(D).astype(np.float32)
        scores = jnp.einsum('hnd,hmd->hnm', q2, k2) * scale + mask[None]
        attn = jax.nn.softmax(scores, axis=-1)
        out = jnp.einsum('hnm,hmd->hnd', attn, v2)
        out = out.transpose(1, 0, 2).reshape(N, OUT_F)
        return out @ wo.T + bo

    def _L0_ffn_ref(x, clip_x, clip_down, w_gate, w_up, w_down):
        import jax, jax.numpy as jnp
        import numpy as np
        QMAX = 127.0

        def _ste_round(v):
            return v + jax.lax.stop_gradient(jnp.round(v) - v)

        def _act_fake_quant(x, clip_factor):
            scale = jax.nn.sigmoid(clip_factor) * jnp.max(jnp.abs(x)) / QMAX
            return jnp.clip(_ste_round(x / scale), -QMAX - 1.0, QMAX) * scale

        def _weight_fake_quant(w):
            scale = jnp.max(jnp.abs(w), axis=1, keepdims=True) / QMAX
            return jnp.clip(_ste_round(w / scale), -QMAX - 1.0, QMAX) * scale
        xq = _act_fake_quant(x, clip_x[0])
        gate = jnp.einsum('bsh,ih->bsi', xq, _weight_fake_quant(w_gate))
        up = jnp.einsum('bsh,ih->bsi', xq, _weight_fake_quant(w_up))
        h = _act_fake_quant(jax.nn.silu(gate) * up, clip_down[0])
        return jnp.einsum('bsi,hi->bsh', h, _weight_fake_quant(w_down))
    edge_index = jnp.stack([src, dst])
    x = x + _L0_gnn_ref(_layernorm(x, axis=-1), edge_index, edge_type_5, L0_gnn_edge_type_weights, L0_gnn_wq, L0_gnn_bq, L0_gnn_wk, L0_gnn_bk, L0_gnn_wv, L0_gnn_bv, L0_gnn_wiq, L0_gnn_biq, L0_gnn_wik, L0_gnn_bik, L0_gnn_wiv, L0_gnn_biv, L0_gnn_wo, L0_gnn_bo)
    x = x + _L0_ffn_ref(_layernorm(x, axis=-1)[None], L0_ffn_clip_x, L0_ffn_clip_down, L0_ffn_w_gate, L0_ffn_w_up, L0_ffn_w_down)[0]
    return x

_drawn_inputs = setup_inputs


def setup_inputs(seed=0):
    import zlib

    import numpy as np

    out = dict(_drawn_inputs(seed))
    spreads = {}
    factors = {'L0_gnn_edge_type_weights': 5.653,
     'L0_gnn_wq': 4.047,
     'L0_gnn_bq': 8.0,
     'L0_gnn_wk': 4.03,
     'L0_gnn_bk': 8.0,
     'L0_gnn_bv': 4.995,
     'L0_gnn_wiq': 4.0,
     'L0_gnn_biq': 8.0,
     'L0_gnn_wik': 4.014,
     'L0_gnn_bik': 8.0,
     'L0_gnn_biv': 3.63}
    for name, (base, spread) in spreads.items():
        noise = np.random.default_rng([zlib.crc32(name.encode()), seed]).standard_normal(out[name].shape)
        drawn = base * np.exp(spread * noise) if base else spread * noise
        out[name] = jnp.asarray(drawn.astype(out[name].dtype))
    for name, factor in factors.items():
        out[name] = (out[name] * factor).astype(out[name].dtype)
    return out
```

```python
from contextlib import ExitStack

import concourse.bass as bass
from concourse import mybir

F32 = mybir.dt.float32
F32R = mybir.dt.float32r
BF16 = mybir.dt.bfloat16
F16 = mybir.dt.float16
I32 = mybir.dt.int32
ALU = mybir.AluOpType
ACT = mybir.ActivationFunctionType
X_AXIS = mybir.AxisListType.X

P = 128
N = 384
NT = N // P
C = 1024
KT = C // P
PAIRS = 8
D = 64
HC = C // 2
E = 6528
EPS = 7
EC = 8 * EPS
I_F = 352
IT = 4
IW = I_F // IT
RING = 4
STAGE = 2
CV, CIV, CQ, CK, CPAIR, CO = 0, 8, 16, 24, 32, 48
CHUNKS = 56
AHEAD = 2
MAGIC = 1.5 * 2.0 ** 23
NO_EDGE = -1e30
QMAX = 127.0
LN_EPS = 1e-5
SCALE = 1.0 / D ** 0.5
BIAS_V, BIAS_Q, BIAS_K, BIAS_IQ, BIAS_IK = (KT * i for i in range(5))
CODE_LOW = -108


def gnn_ffn(nc, x, weights, biases, bias_iv, bias_o, edge_cols, edge_rows, edge_w, clips,
            w_gate_up, w_down, key_rows, down_scale_row, out):
    with ExitStack() as ctx:
        def sb(name, shape, dt):
            return ctx.enter_context(nc.sbuf_tensor(name, shape, dt))

        def sem(name):
            return ctx.enter_context(nc.semaphore(name))

        X = sb("X", [P, NT, C], F32)
        XT = [sb(f"XT{i}", [P, KT, N], F32R) for i in range(2)]
        AT = [sb(f"AT{i}", [P, KT, N], F32R) for i in range(2)]
        QT = [sb(f"QT{i}", [P, KT, N], F32R) for i in range(2)]
        V2 = sb("V2", [P, NT, C], F32)
        stage = sb("stage", [P, STAGE, C], F32)
        ring = [sb(f"ring{i}", [P, RING, C], F32R) for i in range(2)]
        scratch = sb("scratch", [P, 3 * NT * N], F32)
        PT = [[sb(f"PT{h}{i}", [P, NT, N], F32R) for i in range(2)] for h in range(2)]
        QP = [[sb(f"QP{h}{i}", [P, N], F32R) for i in range(2)] for h in range(2)]
        KP = [sb(f"KP{i}", [P, N], F32R) for i in range(2)]
        VP = [sb(f"VP{i}", [P, NT, P], F32R) for i in range(2)]
        guT = sb("guT", [P, KT, 2 * IT, IW], BF16)
        wdT = sb("wdT", [P, IT, C], BF16)
        ident = sb("ident", [P, P], F32)
        wide = sb("wide", [P, 5 * P], BF16)
        tri = sb("tri", [P, P], BF16)
        iota = sb("iota", [P, N], F16)
        ones = sb("ones", [1, P], F32)
        bias = sb("bias", [P, 5 * KT], F32)
        edges = sb("edges", [P, 3, EC], I32)
        edge_row = sb("edge_row", [EC, 2, P], I32)
        key_row = sb("key_row", [EC, P], F32)
        ecol = sb("ecol", [P, 8, EC], F32)
        code_e = sb("code_e", [P, EC], I32)
        dup = sb("dup", [P, EC], F32)
        diag = sb("diag", [P, P], BF16)
        ew = sb("ew", [P, 8, 4], F32)
        clip = sb("clip", [P, 4, 2], F32)
        stats = sb("stats", [P, NT, 2, 6], F32)
        mv = sb("mv", [P, NT, 2], F32)
        rs = sb("rs", [P, 6, NT], F32)
        smx = sb("smx", [P, 4, 2 * NT], F32)
        wsc = sb("wsc", [P, 4, 2 * IT], F32)
        dsc = sb("dsc", [P, 4, KT], F32)
        ds_row = key_row[0:KT, :]
        gmx = sb("gmx", [P, 20], F32)
        PS = ctx.enter_context(nc.psum_tensor("PS", [P, 8, HC], F32))
        PROJ, TPOSE, SCORE, OUT = 0, 2, 4, 6
        ACC = 4

        key_bc = scratch[:, 0:2 * EPS * P].rearrange("p (b e j) -> p b e j", b=2, e=EPS)
        same = scratch[:, 2 * EPS * P:2 * EPS * P + EPS * P // 2].bitcast(BF16).rearrange("p (e j) -> p e j", e=EPS)
        onehot = scratch[:, 0:EPS * N].bitcast(BF16).rearrange("p (e s n) -> p e s n", e=EPS, s=2)
        gu_in = scratch[:, 0:2 * C].rearrange("p (b c) -> p b c", b=2)
        dn_in = scratch[:, 2 * C:2 * C + 2 * I_F].rearrange("p (b c) -> p b c", b=2)
        at = 2 * C + 2 * I_F
        gu_q = scratch[:, at:at + C // 2].bitcast(BF16)
        dn_q = scratch[:, at + C // 2:at + C // 2 + I_F // 2].bitcast(BF16)
        SM = [scratch[:, h * NT * N:(h + 1) * NT * N].rearrange("p (t n) -> p t n", t=NT) for h in range(2)]
        mask = scratch[:, 2 * NT * N:3 * NT * N].rearrange("p (t n) -> p t n", t=NT)
        bo_bc = guT[:, :, :, :].rearrange("p a b c -> p (a b c)")[:, 0:2 * C].bitcast(F32)
        biv_bc = guT[:, :, :, :].rearrange("p a b c -> p (a b c)")[:, 2 * C:4 * C].bitcast(F32)
        xqT = scratch[:, 0:KT * N // 2].bitcast(BF16).rearrange("p (k n) -> p k n", k=KT)
        hid = scratch[:, KT * N // 2:KT * N // 2 + IT * N].rearrange("p (i n) -> p i n", i=IT)
        xq = stage[:, :, :].rearrange("p s c -> p (s c)")[:, 0:NT * C // 2].bitcast(BF16).rearrange(
            "p (t c) -> p t c", t=NT)
        ds_bc = stage[:, 0, :]
        down = stage[:, 1, :].rearrange("p (b c) -> p b c", b=2)
        sig = [V2[0:IW, b, 0:N] for b in range(2)]
        hq = V2[:, 2, 0:IT * N // 2].bitcast(BF16).rearrange("p (i n) -> p i n", i=IT)
        iota_i = scratch[:, 3 * C:3 * C + N].bitcast(I32)
        gu_ps = PS[:, 2, :].bitcast(BF16)[:, 0:KT * IW].rearrange("p (k i) -> p k i", k=KT)
        dn_ps = PS[0:IW, 3, :].bitcast(BF16)[:, 0:IT * P].rearrange("p (i o) -> p i o", i=IT)

        def xq_ps(b):
            return PS[:, b, :].bitcast(BF16)[:, 0:2 * N].rearrange("p (k n) -> p k n", k=2)

        stage_in = [sem(f"stage_in{i}") for i in range(STAGE)]
        w_high = sem("w_high")
        w_low = sem("w_low")
        w_used = sem("w_used")
        x_in = sem("x_in")
        small_in = sem("small_in")
        bc_in = sem("bc_in")
        consts = sem("consts")
        dve_chain = sem("dve_chain")
        act_chain = sem("act_chain")
        var_ready = sem("var_ready")
        root_ready = sem("root_ready")
        y_ready = sem("y_ready")
        t_full = sem("t_full")
        t_high = sem("t_high")
        t_low = sem("t_low")
        proj_high = sem("proj_high")
        proj_low = sem("proj_low")
        acc_free = sem("acc_free")
        keys_made = sem("keys_made")
        keys_out = sem("keys_out")
        key_in = [sem(f"key_in{i}") for i in range(2)]
        key_used = sem("key_used")
        oh_ready = sem("oh_ready")
        oh_used = sem("oh_used")
        diag_ready = sem("diag_ready")
        code_full = sem("code_full")
        ffn_in = [sem(f"ffn_in{i}") for i in range(2)]
        ffn_q = sem("ffn_q")
        ffn_full = sem("ffn_full")
        ffn_evac = sem("ffn_evac")
        s_full = sem("s_full")
        s_seen = sem("s_seen")
        s_free = sem("s_free")
        nb_ready = sem("nb_ready")
        exp_done = sem("exp_done")
        p_ready = sem("p_ready")
        vp_high = sem("vp_high")
        vp_low = sem("vp_low")
        o_full = sem("o_full")
        o_high = sem("o_high")
        o_low = sem("o_low")
        soft_in = sem("soft_in")
        ds_turned = sem("ds_turned")
        ds_made = sem("ds_made")
        dsc_out = sem("dsc_out")
        dsbc_in = sem("dsbc_in")
        red_t = sem("red_t")
        red_m = sem("red_m")
        red_b = sem("red_b")
        xq_ready = sem("xq_ready")
        xqt_full = sem("xqt_full")
        xqt_evac = sem("xqt_evac")
        scales_ready = sem("scales_ready")
        gu_full = sem("gu_full")
        sig_ready = sem("sig_ready")
        gu_free = sem("gu_free")
        hq_ready = sem("hq_ready")
        d_full = sem("d_full")
        d_free = sem("d_free")
        y_out = sem("y_out")
        out_done = sem("out_done")

        class Chain:

            def __init__(self, eng, s):
                self.eng, self.sem, self.n = eng, s, 0

            def link(self, ins):
                ins.then_inc(self.sem, 1)
                self.n = self.n + 1

            def join(self):
                self.eng.wait_ge(self.sem, self.n)

            def step(self, ins):
                self.link(ins)
                self.join()

        block = ctx.enter_context(nc.Block())

        @block.sync
        def _(sp):
            def load(c, slot):
                sp.dma_start(stage[:, slot, :], weights[bass.ds(c, 1), :, :].rearrange("c p n -> p (c n)")
                             ).then_inc(stage_in[slot], 16)

            def load_ffn(s, slot):
                sp.wait_ge(ffn_q, s + 1)
                sp.dma_start(gu_in[0:IW, slot, :], w_gate_up[bass.ds(s, 1), :, :].rearrange("s p n -> p (s n)")
                             ).then_inc(ffn_in[slot], 16)
                sp.dma_start(dn_in[:, slot, :], w_down[bass.ds(s, 1), :, :].rearrange("s p n -> p (s n)")
                             ).then_inc(ffn_in[slot], 16)

            for t in range(NT):
                sp.dma_start(X[:, t, :], x[t * P:(t + 1) * P, :]).then_inc(x_in, 16)
            for c in range(STAGE):
                load(c, c)

            def chunks(first, last):
                with sp.Fori(first // 2, last // 2) as i:
                    for j in range(2):
                        sp.wait_ge(w_low, 2 * i + (j - 1))
                        load(2 * i + j, j)

            chunks(2, 4)
            sp.wait_ge(keys_made, 1)
            sp.dma_start(key_rows, key_row[:, :]).then_inc(keys_out, 16)
            sp.wait_ge(keys_out, 16)
            with sp.Fori(0, 4) as i:
                for j in range(2):
                    sp.wait_ge(key_used, 2 * i + (j + 1))
                    sp.dma_start(key_bc[:, j, :, :],
                                 key_rows[bass.ds((2 * i + j) * EPS, EPS), :].unsqueeze(0).to_broadcast([P, EPS, P])
                                 ).then_inc(key_in[j], 16)
                    sp.wait_ge(w_low, 2 * i + (j + 3))
                    load(2 * i + (j + 4), j)
            chunks(12, 26)
            sp.wait_ge(code_full, 1)
            with sp.Fori(0, 4) as i:
                for j in range(2):
                    load_ffn(2 * i + j, j)
                    sp.wait_ge(w_low, 2 * i + (j + 25))
                    load(2 * i + (j + 26), j)
            chunks(34, 38)
            sp.wait_ge(ds_made, 1)
            sp.dma_start(down_scale_row.rearrange("(s p) -> s p", p=P), ds_row[:, :]).then_inc(dsc_out, 16)
            chunks(38, CHUNKS)
            sp.wait_ge(dsc_out, 16)
            sp.wait_ge(xqt_full, KT // 2)
            sp.dma_start(ds_bc, down_scale_row.rearrange("(a n) -> a n", a=1).to_broadcast([P, C])
                         ).then_inc(dsbc_in, 16)
            for m in range(NT):
                sp.wait_ge(y_out, 2 * m + 2)
                sp.dma_start(out[m * P:(m + 1) * P, :], X[:, m, :]).then_inc(out_done, 16)
            sp.wait_ge(out_done, 16 * NT)

        @block.gpsimd
        def _(pool):
            pool.memset(ident[:, :], 0.0).then_inc(consts, 1)
            pool.memset(wide[:, :], 0.0).then_inc(consts, 1)
            pool.memset(tri[:, :], 1.0).then_inc(consts, 1)
            pool.memset(ones[:, :], 1.0).then_inc(consts, 1)
            pool.wait_ge(consts, 4)
            pool.affine_select(out=ident[:, :], in_=ident[:, :], compare_op=ALU.not_equal, fill=1.0,
                               base=0, pattern=[[-1, P]], channel_multiplier=1).then_inc(consts, 1)
            pool.affine_select(out=wide[:, 2 * P:3 * P], in_=wide[:, 2 * P:3 * P], compare_op=ALU.not_equal,
                               fill=1.0, base=0, pattern=[[-1, P]], channel_multiplier=1).then_inc(consts, 1)
            pool.affine_select(out=tri[:, :], in_=tri[:, :], compare_op=ALU.is_ge,
                               fill=0.0, base=-1, pattern=[[1, P]], channel_multiplier=-1).then_inc(consts, 1)
            pool.iota(iota_i, pattern=[[1, N]], base=0, channel_multiplier=0).then_inc(consts, 1)
            pool.iota(code_e[:, :], pattern=[[4, EC]], base=CODE_LOW + 127,
                      channel_multiplier=0).then_inc(consts, 1)

            def low(c, slot):
                pool.wait_ge(w_high, c + 1)
                pool.tensor_tensor(ring[1][:, slot, :], stage[:, slot % STAGE, :],
                                   ring[0][:, slot, :].bitcast(F32), ALU.subtract).then_inc(w_low, 1)

            with pool.Fori(0, 8) as i:
                for j in range(4):
                    low(4 * i + j, j)
            for c in range(CPAIR, CPAIR + 6):
                low(c, c % RING)

            def pair_v(u):
                pool.wait_ge(vp_high, u + 1)
                pool.tensor_tensor(VP[1][:, :, :], V2[:, :, bass.ds(u * P, P)],
                                   VP[0][:, :, :].bitcast(F32), ALU.subtract).then_inc(vp_low, 1)

            with pool.Fori(0, 3) as i:
                for b in range(2):
                    pair_v(2 * i + b)
                    low(4 * i + (38 + 2 * b), (2 + 2 * b) % RING)
                    low(4 * i + (39 + 2 * b), (3 + 2 * b) % RING)
            pair_v(6)
            low(50, 2)
            low(51, 3)
            pair_v(7)
            for c in range(52, CHUNKS):
                low(c, c % RING)

        @block.scalar
        def _(act):
            chain = Chain(act, act_chain)
            act.dma_start(edge_row[:, :, :], edge_rows).then_inc(small_in, 16)
            act.dma_start(edges[:, :, :], edge_cols).then_inc(small_in, 16)
            act.dma_start(bias[:, :], biases).then_inc(small_in, 16)
            act.dma_start(ew[:, 0, :], edge_w.rearrange("(a n) -> a n", a=1).to_broadcast([P, 4])
                          ).then_inc(small_in, 16)
            act.dma_start(clip[:, 0, :], clips.rearrange("(a n) -> a n", a=1).to_broadcast([P, 2])
                          ).then_inc(small_in, 16)
            act.dma_start(bo_bc, bias_o.rearrange("(a n) -> a n", a=1).to_broadcast([P, C])).then_inc(bc_in, 16)
            act.dma_start(biv_bc, bias_iv.rearrange("(a n) -> a n", a=1).to_broadcast([P, C])).then_inc(bc_in, 16)
            act.wait_ge(var_ready, 1)
            act.activation(rs[:, 1, :], rs[:, 0, :], ACT.Sqrt).then_inc(root_ready, 1)

            def high(c2, c, slot):
                act.wait_ge(stage_in[slot % STAGE], 16 * (c2 + 1))
                act.wait_ge(w_used, c + 1)
                act.activation(ring[0][:, slot, :], stage[:, slot % STAGE, :], ACT.Copy).then_inc(w_high, 1)

            def t_take(tau, b, dst):
                act.wait_ge(t_full, tau + 1)
                act.activation(dst, PS[:, TPOSE + b, 0:N], ACT.Copy).then_inc(t_high, 1)

            high(0, 0, 0)
            high(0, 1, 1)
            for k in range(KT):
                t_take(k, k % 2, XT[0][:, k, :])
            act.wait_ge(small_in, 5 * 16)
            chain.step(act.activation(ew[:, 1, :], ew[:, 0, :], ACT.Abs))
            chain.step(act.activation(ew[:, 2, :], ew[:, 1, :], ACT.Exp, scale=-1.0))
            act.activation(ew[:, 3, :], ew[:, 2, :], ACT.Ln, bias=1.0).then_inc(soft_in, 1)
            act.activation(clip[:, 1, :], clip[:, 0, :], ACT.Exp, scale=-1.0).then_inc(soft_in, 1)

            def early(dst, chunk0, bias0, extra=None):
                with act.Fori(0, 2) as i:
                    for j in range(4):
                        high(2 * i + ((chunk0 + AHEAD + j) // 2), 4 * i + (chunk0 + AHEAD + j), (j + AHEAD) % RING)
                        act.wait_ge(w_used, 4 * i + (RING + chunk0 + j + 1))
                        act.activation(dst[0][:, bass.ds(4 * i + j, 1), :].rearrange("p k n -> p (k n)"),
                                       PS[:, PROJ + j % 2, 0:N], ACT.Identity,
                                       bias=bias[:, bass.ds(4 * i + (bias0 + j), 1)]).then_inc(proj_high, 1)
                        if extra:
                            extra(4 * i + j)

            early(AT, CV, BIAS_V)
            with act.Fori(0, 2) as i:
                for j in range(4):
                    high(2 * i + ((CIV + AHEAD + j) // 2), 4 * i + (CIV + AHEAD + j), (j + AHEAD) % RING)
            early(QT, CQ, BIAS_Q)

            def ffn_take(s):
                act.wait_ge(ffn_full, s + 1)
                act.activation(guT[:, :, bass.ds(s, 1), :].rearrange("p k s i -> p k (s i)"),
                               gu_ps, ACT.Copy)
                act.activation(wdT[0:IW, :, bass.ds(s * P, P)], dn_ps, ACT.Copy).then_inc(ffn_evac, 1)

            early(AT, CK, BIAS_K, ffn_take)

            def q_high(t):
                act.wait_ge(w_used, 2 * t + (RING + CPAIR + 1))
                for h in range(2):
                    r = slice(h * D, h * D + D)
                    ins = act.activation(QP[h][0][r, :], PS[r, PROJ, 0:N], ACT.Identity,
                                         bias=bias[r, bass.ds(t + BIAS_IQ, 1)])
                ins.then_inc(proj_high, 1)

            def k_high(t):
                act.wait_ge(w_used, 2 * t + (RING + CPAIR + 2))
                act.activation(KP[0][:, :], PS[:, PROJ + 1, 0:N], ACT.Identity,
                               bias=bias[:, bass.ds(t + BIAS_IK, 1)]).then_inc(proj_high, 1)

            def v_high(u):
                act.wait_ge(o_full, 2 * u + 1)
                act.activation(VP[0][:, :, :], V2[:, :, bass.ds(u * P, P)],
                               ACT.Copy).then_inc(vp_high, 1)

            def exps(p, h):
                act.wait_ge(nb_ready, 2 * p + (h + 1))
                for m in range(NT):
                    ins = act.activation(SM[h][:, m, :], SM[h][:, m, :], ACT.Exp, scale=SCALE,
                                         bias=smx[:, 1, h * NT + m:h * NT + m + 1],
                                         accum_out=smx[:, 2, h * NT + m:h * NT + m + 1])
                ins.then_inc(exp_done, 1)

            def o_take(u, h):
                r = slice(h * D, h * D + D)
                act.wait_ge(o_full, 2 * u + (h + 2))
                act.activation(XT[0][r, bass.ds(u, 1), :].rearrange("p k n -> p (k n)"),
                               PS[r, OUT + h, 0:N], ACT.Copy).then_inc(o_high, 1)

            def probs_high(u):
                for h in range(2):
                    for m in range(NT):
                        t_take(6 * u + (8 + 3 * h + m), (h * NT + m) % 2, PT[h][0][:, m, :])

            high(17, 34, 2)
            q_high(0)
            high(17, 35, 3)
            k_high(0)
            exps(0, 0)
            q_high(1)
            exps(0, 1)
            high(18, 36, 0)
            high(18, 37, 1)
            k_high(1)

            def pair(u, split, project, score=True):
                v_high(u)
                probs_high(u)
                if split:
                    high(*split[0])
                o_take(u, 0)
                if score:
                    exps(u + 1, 0)
                if project:
                    q_high(u + 2)
                if score:
                    exps(u + 1, 1)
                o_take(u, 1)
                if split:
                    high(*split[1])
                if project:
                    k_high(u + 2)

            with act.Fori(0, 3) as i:
                for b in range(2):
                    pair(2 * i + b, [(2 * i + (19 + b), 4 * i + (38 + 2 * b), (2 + 2 * b) % RING),
                                     (2 * i + (19 + b), 4 * i + (39 + 2 * b), (3 + 2 * b) % RING)], True)
            pair(6, [(25, 50, 2), (25, 51, 3)], False)
            pair(7, None, False, False)
            for c in range(52, 56):
                high(c // 2, c, c % RING)
            act.wait_ge(var_ready, 2)
            act.activation(rs[:, 1, :], rs[:, 0, :], ACT.Sqrt).then_inc(root_ready, 1)
            for k in range(KT // 2):
                act.wait_ge(xqt_full, k + 1)
                act.activation(xqT[:, 2 * k:2 * k + 2, :], xq_ps(k % 2), ACT.Copy).then_inc(xqt_evac, 1)
            act.wait_ge(scales_ready, 1)
            for i in range(IT):
                act.wait_ge(gu_full, i + 1)
                act.activation(sig[i % 2], PS[0:IW, 2 * (i % 2), 0:N], ACT.Exp,
                               scale=wsc[0:IW, 3, i:i + 1]).then_inc(sig_ready, 1)

        @block.tensor
        def _(pe):
            pe.sem_inc(w_used, RING)
            pe.sem_inc(oh_used, EPS)
            pe.sem_inc(o_full, 1)
            pe.wait_ge(consts, 9)

            def turn(tau, b, src):
                pe.wait_ge(t_low, tau + 1)
                for m in range(NT):
                    ins = pe.transpose(PS[:, TPOSE + b, m * P:(m + 1) * P], src(m), ident[:, :])
                ins.then_inc(t_full, 1)

            for k in range(KT):
                if k == 0:
                    pe.wait_ge(y_ready, NT)
                turn(k, k % 2, lambda m: V2[:, m, k * P:(k + 1) * P])

            def passes(outs, lhs, rhs, start, stop):
                for n, (a, b) in enumerate(((0, 0), (0, 1), (1, 0))):
                    ins = pe.matmul(outs, lhs[a], rhs[b], start=start and n == 0, stop=stop and n == 2,
                                    skip_group_check=True)
                return ins

            def begin(c, a):
                pe.wait_ge(w_low, c + 1)
                if a is not None:
                    pe.wait_ge(proj_low, a + 1)

            def part(slot, bank, src, ks):
                w = [ring[i][:, slot, :].rearrange("p (k o) -> p k o", k=KT) for i in range(2)]
                for k in ks:
                    ins = passes(PS[:, PROJ + bank, 0:N], [w[i][:, k, :] for i in range(2)],
                                 [src[i][:, k, :] for i in range(2)], k == 0, k == KT - 1)
                return ins

            def finish(ins):
                ins.then_inc(w_used, 1)

            def project(c, a, slot, src):
                begin(c, a)
                finish(part(slot, slot % 2, src, range(KT)))

            pe.wait_ge(t_low, KT + 2)
            with pe.Fori(0, 2) as i:
                for j in range(4):
                    project(4 * i + j, 4 * i + j, j, XT)

            def wide_product(chunk0, src, turn0):
                with pe.Fori(0, 2) as i:
                    pe.wait_ge(acc_free, i + (turn0 + 1))
                    for j in range(4):
                        pe.wait_ge(w_low, 4 * i + (chunk0 + j + 1))
                        w = [ring[s][:, j, :].rearrange("p (k o) -> p k o", k=2) for s in range(2)]
                        for k2 in range(2):
                            k = 2 * j + k2
                            for m in range(NT):
                                ins = passes(PS[:, ACC + m, :], [src[s][:, k, m * P:(m + 1) * P] for s in range(2)],
                                             [w[s][:, k2, :] for s in range(2)], k == 0, k == KT - 1)
                        ins.then_inc(w_used, 1)

            pe.wait_ge(proj_low, 8 + 2)
            wide_product(CIV, AT, 0)

            pe.wait_ge(acc_free, 3)
            pe.wait_ge(diag_ready, 1)
            for s in range(NT):
                pe.matmul(PS[:, ACC + s, 0:N], diag[:, :], wide[:, (2 - s) * P:(5 - s) * P], start=True, stop=False,
                          skip_group_check=True)

            def edge(e, slot):
                pe.wait_ge(oh_ready, e + 1)
                for s in range(NT):
                    ins = pe.matmul(PS[:, ACC + s, 0:N], onehot[:, slot, 0, s * P:(s + 1) * P],
                                    onehot[:, slot, 1, :], start=False, stop=False, skip_group_check=True)
                ins.then_inc(oh_used, 1)

            with pe.Fori(0, 2) as i:
                for j in range(4):
                    project(4 * i + (CQ + j), 4 * i + (8 + j), j, XT)
                    for s in range(EPS):
                        edge(4 * EPS * i + (j * EPS + s), s)
            for s in range(NT):
                ins = pe.matmul(PS[:, ACC + s, 0:N], wide[:, 0:P], wide[:, 0:N], start=False, stop=True,
                                skip_group_check=True)
            ins.then_inc(code_full, 1)

            def ffn_turn(s):
                pe.wait_ge(ffn_q, s + 3)
                pe.wait_ge(ffn_evac, s + 1)
                for k in range(KT):
                    pe.transpose(gu_ps[:, k, :], gu_q[0:IW, k * P:(k + 1) * P], wide[0:IW, 2 * P:2 * P + IW])
                for i4 in range(IT):
                    ins = pe.transpose(dn_ps[:, i4, :], dn_q[:, i4 * IW:(i4 + 1) * IW], wide[:, 2 * P:3 * P])
                ins.then_inc(ffn_full, 1)

            with pe.Fori(0, 2) as i:
                for j in range(4):
                    project(4 * i + (CK + j), 4 * i + (16 + j), j, XT)
                    ffn_turn(4 * i + j)

            pe.wait_ge(proj_low, 24 + 2)
            pe.wait_ge(ffn_evac, 8 + 1)
            pe.transpose(PS[0:KT, TPOSE, 0:P], dsc[:, 1, :], ident[:, :]).then_inc(ds_turned, 1)

            def score(p, m):
                for h in range(2):
                    pe.wait_ge(s_free, 6 * p + (2 * m + h + 1))
                    passes(PS[:, SCORE + h, 0:N], [QP[h][s][:, m * P:(m + 1) * P] for s in range(2)],
                           [KP[s][:, :] for s in range(2)], True, True).then_inc(s_full, 1)

            def turn_probs(u, h, m):
                if m == 0:
                    pe.wait_ge(p_ready, 2 * u + (h + 1))
                turn(6 * u + (8 + 3 * h + m), (h * NT + m) % 2,
                     lambda n: SM[h][:, n, m * P:(m + 1) * P])

            def weigh(u, h):
                pe.wait_ge(vp_low, u + 1)
                pe.wait_ge(t_low, 6 * u + (8 + 3 * h + 3 + 2))
                pe.wait_ge(o_low, 2 * u + (h + 1))
                for m in range(NT):
                    ins = passes(PS[:, OUT + h, 0:N], [VP[s][:, m, :] for s in range(2)],
                                 [PT[h][s][:, m, :] for s in range(2)], m == 0, m == NT - 1)
                ins.then_inc(o_full, 1)

            project(32, 24, 0, QT)
            project(33, 25, 1, AT)
            pe.wait_ge(proj_low, 26 + 2)
            begin(34, 26)
            score(0, 0)
            part(2, 0, QT, range(0, 4))
            score(0, 1)
            finish(part(2, 0, QT, range(4, 8)))
            score(0, 2)
            project(35, 27, 3, AT)

            def pair(u, c0, slot0, scores=True, proj=True):
                a0 = 2 * u + 28
                turn_probs(u, 0, 0)
                turn_probs(u, 0, 1)
                if proj:
                    begin(c0, a0)
                    part(slot0, 0, QT, range(0, 3))
                turn_probs(u, 0, 2)
                turn_probs(u, 1, 0)
                if proj:
                    part(slot0, 0, QT, range(3, 6))
                turn_probs(u, 1, 1)
                turn_probs(u, 1, 2)
                if proj:
                    finish(part(slot0, 0, QT, range(6, 8)))
                if scores:
                    pe.wait_ge(proj_low, a0 + 2)
                    score(u + 1, 0)
                weigh(u, 0)
                if scores:
                    score(u + 1, 1)
                if proj:
                    begin(c0 + 1, a0 + 1)
                    part(slot0 + 1, 1, AT, range(0, 3))
                if scores:
                    score(u + 1, 2)
                if proj:
                    part(slot0 + 1, 1, AT, range(3, 6))
                weigh(u, 1)
                if proj:
                    finish(part(slot0 + 1, 1, AT, range(6, 8)))

            with pe.Fori(0, 3) as i:
                for b in range(2):
                    pair(2 * i + b, 4 * i + (36 + 2 * b), 2 * b)
            pair(6, None, None, True, False)
            pair(7, None, None, False, False)

            pe.wait_ge(o_low, 16 + 2)
            wide_product(CO, XT, 2)

            def reduce_max(n, col):
                pe.wait_ge(red_t, n + 1)
                rows = col.shape[0]
                pe.transpose(PS[0:1, TPOSE, 0:rows], col, ident[0:rows, 0:rows]).then_inc(red_b, 1)
                pe.wait_ge(red_m, n + 1)
                pe.matmul(PS[:, TPOSE + 1, 0:1], ones[:, :], gmx[0:1, 8:9], start=True, stop=True).then_inc(red_b, 1)

            reduce_max(0, gmx[:, 0:1])
            for k in range(KT // 2):
                pe.wait_ge(xq_ready, k // 2 * NT + NT)
                if k >= 2:
                    pe.wait_ge(xqt_evac, k - 1)
                for k2 in range(2):
                    for m in range(NT):
                        kk = (2 * k + k2)
                        ins = pe.transpose(xq_ps(k % 2)[:, k2, m * P:(m + 1) * P],
                                           xq[:, m, kk * P:(kk + 1) * P], wide[:, 2 * P:3 * P])
                ins.then_inc(xqt_full, 1)
            pe.wait_ge(xqt_evac, KT // 2)
            for i in range(IT):
                if i >= 2:
                    pe.wait_ge(gu_free, i - 1)
                for g in range(2):
                    for k in range(KT):
                        ins = pe.matmul(PS[0:IW, 2 * (i % 2) + g, 0:N], guT[:, k, g * IT + i, :], xqT[:, k, :],
                                        start=(k == 0), stop=(k == KT - 1))
                ins.then_inc(gu_full, 1)
            reduce_max(1, gmx[0:IW, 4:5])
            for m in range(NT):
                for hf in range(2):
                    t = 2 * m + hf
                    if t == 0:
                        pe.wait_ge(hq_ready, 1)
                    if t >= 4:
                        pe.wait_ge(d_free, t - 3)
                    for i in range(IT):
                        ins = pe.matmul(PS[:, 4 + t % 4, :], hq[0:IW, i, m * P:(m + 1) * P],
                                        wdT[0:IW, i, hf * HC:(hf + 1) * HC], start=(i == 0), stop=(i == IT - 1))
                    ins.then_inc(d_full, 1)

        @block.vector
        def _(dve):
            chain = Chain(dve, dve_chain)
            dve.sem_inc(t_low, 2)
            dve.sem_inc(proj_low, 2)
            dve.sem_inc(acc_free, 1)
            dve.sem_inc(key_used, 2)
            dve.sem_inc(ffn_q, 2)
            dve.sem_inc(ffn_evac, 1)
            dve.sem_inc(s_free, 2)
            dve.sem_inc(o_low, 2)
            for h in range(2):
                r = slice((1 - h) * D, (1 - h) * D + D)
                for s in range(2):
                    chain.link(dve.memset(QP[h][s][r, :].bitcast(F32), 0.0))
            dve.wait_ge(small_in, 5 * 16)
            dve.scalar_tensor_tensor(key_row[:, :], edge_row[:, 0, :], float(N), edge_row[:, 1, :],
                                     ALU.mult, ALU.add).then_inc(keys_made, 1)
            SRC, DST, KEY, TYP, NEG, VAL = range(6)
            chain.link(dve.tensor_copy(ecol[:, SRC, :], edges[:, 0, :]))
            chain.link(dve.tensor_copy(ecol[:, DST, :], edges[:, 1, :]))
            chain.step(dve.tensor_scalar(ecol[:, TYP, :], edges[:, 2, :], 4.0, -1.0, ALU.min, ALU.add))
            chain.link(dve.scalar_tensor_tensor(ecol[:, KEY, :], ecol[:, SRC, :], float(N), ecol[:, DST, :],
                                                ALU.mult, ALU.add))
            chain.step(dve.tensor_scalar(ecol[:, NEG, :], ecol[:, TYP, :], 0.0, 4.0, ALU.is_lt, ALU.mult))
            chain.step(dve.tensor_tensor(ecol[:, TYP, :], ecol[:, TYP, :], ecol[:, NEG, :], ALU.add))
            chain.step(dve.tensor_scalar(ecol[:, TYP, :], ecol[:, TYP, :], 0.25, 1.0, ALU.mult, ALU.add))
            dve.wait_ge(consts, 9)
            chain.step(dve.tensor_scalar(code_e[:, :], code_e[:, :], 23, None, ALU.logical_shift_left))
            chain.link(dve.tensor_tensor(ecol[:, VAL, :], ecol[:, TYP, :], code_e[:, :].bitcast(F32), ALU.mult))
            chain.link(dve.tensor_copy(iota[:, :], iota_i))
            dve.tensor_scalar(diag[:, :], ident[:, :], 1.75 * 2.0 ** (CODE_LOW - 4), None,
                              ALU.mult).then_inc(diag_ready, 1)

            def norm(n):
                for m in range(NT):
                    if n == 0:
                        dve.wait_ge(x_in, 16 * NT)
                    for g in range(2):
                        chain.link(dve.bn_stats(stats[:, m, g, :], X[:, m, g * HC:(g + 1) * HC]))
                    chain.join()
                    chain.link(dve.bn_aggr(mv[:, m, :], stats[:, m, :, :].rearrange("p a b -> p (a b)")))
                chain.join()
                dve.tensor_scalar(rs[:, 0, :], mv[:, :, 1], LN_EPS, None, ALU.add).then_inc(var_ready, 1)
                dve.wait_ge(root_ready, n + 1)
                chain.step(dve.reciprocal(rs[:, 2, :], rs[:, 1, :]))
                chain.step(dve.tensor_tensor(rs[:, 3, :], rs[:, 0, :], rs[:, 2, :], ALU.mult))
                chain.step(dve.scalar_tensor_tensor(rs[:, 4, :], rs[:, 1, :], 1.0, rs[:, 3, :], ALU.mult, ALU.add))
                chain.step(dve.tensor_scalar(rs[:, 5, :], rs[:, 4, :], 0.5, None, ALU.mult))
                chain.step(dve.reciprocal(rs[:, 2, :], rs[:, 5, :]))
                for m in range(NT):
                    ins = dve.tensor_scalar(V2[:, m, :], X[:, m, :], mv[:, m, 0:1], rs[:, 2, m:m + 1],
                                            ALU.subtract, ALU.mult)
                    ins.then_inc(y_ready, 1)

            norm(0)

            def t_rest(tau, b, high, low):
                dve.wait_ge(t_high, tau + 1)
                dve.tensor_tensor(low, PS[:, TPOSE + b, 0:N], high.bitcast(F32), ALU.subtract).then_inc(t_low, 1)

            for k in range(KT):
                t_rest(k, k % 2, XT[0][:, k, :], XT[1][:, k, :])

            def tile_low(a, k, b, dst, col):
                dve.wait_ge(proj_high, a + 1)
                at_k = [dst[s][:, bass.ds(k, 1), :].rearrange("p k n -> p (k n)") for s in range(2)]
                dve.scalar_tensor_tensor(at_k[1], PS[:, PROJ + b, 0:N], bias[:, bass.ds(col, 1)],
                                         at_k[0].bitcast(F32), ALU.add, ALU.subtract).then_inc(proj_low, 1)

            base = chain.n
            with dve.Fori(0, 2) as i:
                for j in range(4):
                    s = 4 * i + j
                    chain.n = 8 * i + (base + 2 * j)
                    dve.wait_ge(key_in[j % 2], 32 * i + 16 * (j // 2 + 1))
                    cols = bass.ds(s * EPS, EPS)
                    dve.wait_ge(key_used, s + 2)
                    chain.step(dve.tensor_tensor(same[:, :, :], key_bc[:, j % 2, :, :],
                                                 ecol[:, KEY, cols].unsqueeze(2).to_broadcast([P, EPS, P]),
                                                 ALU.is_equal))
                    chain.step(dve.tensor_tensor(same[:, :, :], same[:, :, :],
                                                 tri[:, :].unsqueeze(1).to_broadcast([P, EPS, P]), ALU.mult))
                    dve.tensor_reduce(dup[:, cols], same[:, :, :], X_AXIS, ALU.max).then_inc(key_used, 1)
                    tile_low(4 * i + j, s, j % 2, AT, s + BIAS_V)
            chain.n = base + 16
            dve.wait_ge(key_used, 8 + 2)
            chain.step(dve.tensor_scalar(dup[:, :], dup[:, :], -1.0, 1.0, ALU.mult, ALU.add))
            chain.step(dve.tensor_tensor(ecol[:, VAL, :], ecol[:, VAL, :], dup[:, :], ALU.mult))
            dve.wait_ge(bc_in, 32)
            for m in range(NT):
                chain.link(dve.tensor_tensor(X[:, m, :], X[:, m, :], bo_bc, ALU.add))
            with dve.Fori(0, 2) as i:
                dve.wait_ge(w_used, 4 * i + (RING + CIV + 4))
                for m in range(NT):
                    ins = dve.tensor_tensor(V2[:, m, bass.ds(i * HC, HC)], PS[:, ACC + m, :],
                                            biv_bc[:, bass.ds(i * HC, HC)], ALU.add)
                ins.then_inc(acc_free, 1)

            with dve.Fori(0, 2) as i:
                for j in range(4):
                    for s in range(EPS):
                        e = 4 * EPS * i + (j * EPS + s)
                        dve.wait_ge(oh_used, e + 1)
                        dve.tensor_scalar(onehot[:, s, 0, :], iota[:, :], ecol[:, SRC, bass.ds(e, 1)],
                                          ecol[:, VAL, bass.ds(e, 1)], ALU.is_equal, ALU.mult)
                        dve.tensor_scalar(onehot[:, s, 1, :], iota[:, :], ecol[:, DST, bass.ds(e, 1)],
                                          None, ALU.is_equal).then_inc(oh_ready, 1)
                    tile_low(4 * i + (8 + j), 4 * i + j, j % 2, QT, 4 * i + (BIAS_Q + j))

            def to_ints(src, q, sc, s, rows):
                r = slice(0, rows)
                c = bass.ds(s, 1)
                chain.step(dve.tensor_reduce(sc[r, 0, c], src, X_AXIS, ALU.max, apply_absolute_value=True))
                chain.step(dve.tensor_scalar(sc[r, 1, c], sc[r, 0, c], 1.0 / QMAX, None, ALU.mult))
                chain.step(dve.reciprocal(sc[r, 2, c], sc[r, 1, c]))
                chain.step(dve.tensor_scalar(src, src, sc[r, 2, c], MAGIC, ALU.mult, ALU.add))
                return dve.tensor_scalar(q, src, MAGIC, None, ALU.subtract)

            base = chain.n
            with dve.Fori(0, 2) as i:
                for j in range(4):
                    s = 4 * i + j
                    chain.n = 32 * i + (base + 8 * j)
                    dve.wait_ge(ffn_in[j % 2], 64 * i + 32 * (j // 2 + 1))
                    dve.wait_ge(ffn_evac, s + 1)
                    to_ints(gu_in[0:IW, j % 2, :], gu_q[0:IW, :], wsc, s, IW)
                    to_ints(dn_in[:, j % 2, :], dn_q, dsc, s, P).then_inc(ffn_q, 1)
                    tile_low(4 * i + (16 + j), s, j % 2, AT, s + BIAS_K)
            chain.n = base + 64

            dve.wait_ge(soft_in, 2)
            chain.step(dve.scalar_tensor_tensor(ew[:, 4, :], ew[:, 0, :], 0.0, ew[:, 3, :], ALU.max, ALU.add))
            chain.step(dve.tensor_scalar(ew[:, 5, :], ew[:, 4, :], 1.0 / SCALE, None, ALU.mult))
            chain.step(dve.tensor_scalar(clip[:, 2, :], clip[:, 1, :], 1.0, None, ALU.add))
            chain.step(dve.reciprocal(clip[:, 3, :], clip[:, 2, :]))
            chain.step(dve.tensor_scalar(clip[:, 2, :], clip[:, 3, :], 1.0 / QMAX, None, ALU.mult))
            code = PS[:, ACC:ACC + NT, 0:N]
            dve.wait_ge(code_full, 1)
            dve.wait_ge(ffn_full, 8)
            kind = SM[0].bitcast(I32)
            chain.step(dve.tensor_scalar(kind, code.bitcast(I32), 21, 3, ALU.logical_shift_right, ALU.bitwise_and))
            chain.step(dve.tensor_scalar(mask, code, 0.0, NO_EDGE, ALU.is_equal, ALU.mult))
            for w in range(4):
                chain.step(dve.tensor_scalar(SM[1], kind, float(w), ew[:, 5, w:w + 1], ALU.is_equal, ALU.mult))
                chain.step(dve.tensor_tensor(mask, mask, SM[1], ALU.add))

            dve.wait_ge(ds_turned, 1)
            dve.tensor_copy(ds_row[:, :], PS[0:KT, TPOSE, 0:P]).then_inc(ds_made, 1)

            def q_low(t):
                dve.wait_ge(proj_high, 2 * t + 25)
                for h in range(2):
                    r = slice(h * D, h * D + D)
                    ins = dve.scalar_tensor_tensor(QP[h][1][r, :], PS[r, PROJ, 0:N], bias[r, bass.ds(t + BIAS_IQ, 1)],
                                                   QP[h][0][r, :].bitcast(F32), ALU.add, ALU.subtract)
                ins.then_inc(proj_low, 1)

            def k_low(t):
                dve.wait_ge(proj_high, 2 * t + 26)
                dve.scalar_tensor_tensor(KP[1][:, :], PS[:, PROJ + 1, 0:N], bias[:, bass.ds(t + BIAS_IK, 1)],
                                         KP[0][:, :].bitcast(F32), ALU.add, ALU.subtract).then_inc(proj_low, 1)

            def masked(p, m):
                for h in range(2):
                    dve.wait_ge(s_full, 6 * p + (2 * m + h + 1))
                    dve.sem_inc(s_seen, 1)
                    dve.tensor_tensor_reduce(SM[h][:, m, :], PS[:, SCORE + h, 0:N], mask[:, m, :], 1.0, -3e38,
                                             ALU.add, ALU.max, smx[:, 0, h * NT + m:h * NT + m + 1]
                                             ).then_inc(s_free, 1)

            def negate(p):
                dve.wait_ge(s_free, 6 * p + (6 + 2))
                for h in range(2):
                    hs = slice(h * NT, (h + 1) * NT)
                    dve.tensor_scalar(smx[:, 1, hs], smx[:, 0, hs], -SCALE, None, ALU.mult).then_inc(nb_ready, 1)

            def normalise(p, h):
                hs = slice(h * NT, (h + 1) * NT)
                dve.wait_ge(exp_done, 2 * p + (h + 1))
                chain.step(dve.reciprocal(smx[:, 3, hs], smx[:, 2, hs]))
                for m in range(NT):
                    ins = dve.tensor_scalar(SM[h][:, m, :], SM[h][:, m, :], smx[:, 3, h * NT + m:h * NT + m + 1],
                                            None, ALU.mult)
                ins.then_inc(p_ready, 1)

            def o_rest(u, h):
                r = slice(h * D, h * D + D)
                at_u = [XT[s][r, bass.ds(u, 1), :].rearrange("p k n -> p (k n)") for s in range(2)]
                dve.wait_ge(o_high, 2 * u + (h + 1))
                dve.tensor_tensor(at_u[1], PS[r, OUT + h, 0:N], at_u[0].bitcast(F32), ALU.subtract
                                  ).then_inc(o_low, 1)

            q_low(0)
            k_low(0)
            masked(0, 0)
            masked(0, 1)
            masked(0, 2)
            negate(0)
            q_low(1)
            normalise(0, 0)
            normalise(0, 1)
            k_low(1)

            def pair(u, scores=True, proj=True):
                for h in range(2):
                    for m in range(NT):
                        t_rest(6 * u + (8 + 3 * h + m), (h * NT + m) % 2, PT[h][0][:, m, :], PT[h][1][:, m, :])
                if scores:
                    masked(u + 1, 0)
                    masked(u + 1, 1)
                    masked(u + 1, 2)
                    negate(u + 1)
                o_rest(u, 0)
                if proj:
                    q_low(u + 2)
                if scores:
                    normalise(u + 1, 0)
                    normalise(u + 1, 1)
                o_rest(u, 1)
                if proj:
                    k_low(u + 2)

            base = chain.n
            with dve.Fori(0, 3) as i:
                for b in range(2):
                    chain.n = 4 * i + (base + 2 * b)
                    pair(2 * i + b)
            chain.n = base + 12
            pair(6, True, False)
            pair(7, False, False)

            with dve.Fori(0, 2) as i:
                dve.wait_ge(w_used, 4 * i + (RING + CO + 4))
                for m in range(NT):
                    ins = dve.tensor_tensor(X[:, m, bass.ds(i * HC, HC)], PS[:, ACC + m, :],
                                            X[:, m, bass.ds(i * HC, HC)], ALU.add)
                ins.then_inc(acc_free, 1)
            dve.wait_ge(acc_free, 5)

            norm(1)
            dve.wait_ge(y_ready, 2 * NT)

            def greatest(n, cols, col):
                chain.join()
                dve.tensor_reduce(gmx[0:cols.shape[0], col:col + 1], cols, X_AXIS, ALU.max).then_inc(red_t, 1)
                dve.wait_ge(red_b, 2 * n + 1)
                dve.tensor_reduce(gmx[0:1, 8:9], PS[0:1, TPOSE, 0:cols.shape[0]], X_AXIS, ALU.max).then_inc(red_m, 1)
                dve.wait_ge(red_b, 2 * n + 2)
                chain.step(dve.tensor_tensor(gmx[:, 9 + n:10 + n], PS[:, TPOSE + 1, 0:1], clip[:, 2, n:n + 1], ALU.mult))
                chain.step(dve.reciprocal(gmx[:, 11 + n:12 + n], gmx[:, 9 + n:10 + n]))

            for m in range(NT):
                chain.link(dve.tensor_reduce(gmx[:, 1 + m:2 + m], V2[:, m, :], X_AXIS, ALU.max,
                                             apply_absolute_value=True))
            greatest(0, gmx[:, 1:4], 0)

            def quantise(src, dst, col):
                chain.step(dve.tensor_scalar(src, src, gmx[:src.shape[0], col:col + 1], QMAX, ALU.mult, ALU.min))
                chain.step(dve.tensor_scalar(src, src, -QMAX - 1.0, MAGIC, ALU.max, ALU.add))
                return dve.tensor_scalar(dst, src, MAGIC, None, ALU.subtract)

            for hf in range(2):
                for m in range(NT):
                    quantise(V2[:, m, hf * HC:(hf + 1) * HC], xq[:, m, hf * HC:(hf + 1) * HC], 11
                             ).then_inc(xq_ready, 1)
            chain.step(dve.tensor_scalar(wsc[0:IW, 2, :], wsc[0:IW, 1, :], gmx[0:IW, 9:10], None, ALU.mult))
            dve.tensor_scalar(wsc[0:IW, 3, :], wsc[0:IW, 2, :], -1.0, None, ALU.mult).then_inc(scales_ready, 1)
            for i in range(IT):
                g, u = PS[0:IW, 2 * (i % 2), 0:N], PS[0:IW, 2 * (i % 2) + 1, 0:N]
                ht = hid[0:IW, i, :]
                dve.wait_ge(sig_ready, i + 1)
                chain.step(dve.tensor_scalar(sig[i % 2], sig[i % 2], 1.0, None, ALU.add))
                chain.step(dve.reciprocal(sig[i % 2], sig[i % 2]))
                chain.step(dve.scalar_tensor_tensor(ht, g, wsc[0:IW, 2, i:i + 1], sig[i % 2], ALU.mult, ALU.mult))
                dve.scalar_tensor_tensor(ht, u, wsc[0:IW, 2, IT + i:IT + i + 1], ht, ALU.mult, ALU.mult
                                         ).then_inc(gu_free, 1)
                dve.wait_ge(gu_free, i + 1)
                chain.link(dve.tensor_reduce(gmx[0:IW, 16 + i:17 + i], ht, X_AXIS, ALU.max, apply_absolute_value=True))
            chain.join()
            greatest(1, gmx[0:IW, 16:20], 4)
            quantise(hid[0:IW, :, :], hq[0:IW, :, :], 12).then_inc(hq_ready, 1)
            dve.wait_ge(dsbc_in, 16)
            for m in range(NT):
                for hf in range(2):
                    t = 2 * m + hf
                    cs = slice(hf * HC, (hf + 1) * HC)
                    dve.wait_ge(d_full, t + 1)
                    if t >= 2:
                        dve.wait_ge(y_out, t - 1)
                    dve.scalar_tensor_tensor(down[:, hf, :], PS[:, 4 + t % 4, :], gmx[:, 10:11],
                                             ds_bc[:, cs], ALU.mult, ALU.mult).then_inc(d_free, 1)
                    dve.wait_ge(d_free, t + 1)
                    dve.tensor_tensor(X[:, m, cs], X[:, m, cs], down[:, hf, :], ALU.add).then_inc(y_out, 1)


NAMES = ["x", "weights", "biases", "bias_iv", "bias_o", "edge_cols", "edge_rows", "edge_w", "clips",
         "w_gate_up", "w_down"]


def layout(x, src, dst, edge_type_5, L0_gnn_edge_type_weights, L0_gnn_wq, L0_gnn_bq, L0_gnn_wk, L0_gnn_bk,
           L0_gnn_wv, L0_gnn_bv, L0_gnn_wiq, L0_gnn_biq, L0_gnn_wik, L0_gnn_bik, L0_gnn_wiv, L0_gnn_biv,
           L0_gnn_wo, L0_gnn_bo, L0_ffn_clip_x, L0_ffn_clip_down, L0_ffn_w_gate, L0_ffn_w_up, L0_ffn_w_down):
    import numpy as np

    def tiles(w):
        return np.asarray(w).reshape(KT, P, KT, P).transpose(0, 3, 2, 1).reshape(KT, P, C)

    def halves(w):
        return np.asarray(w).reshape(2, HC, 4, 2, P).transpose(0, 2, 4, 3, 1).reshape(8, P, C)

    pairs = np.stack([tiles(L0_gnn_wiq), tiles(L0_gnn_wik)], axis=1).reshape(16, P, C)
    weights = np.concatenate([tiles(L0_gnn_wv), halves(L0_gnn_wiv), tiles(L0_gnn_wq), tiles(L0_gnn_wk), pairs,
                              halves(L0_gnn_wo)])
    biases = np.concatenate([np.asarray(b).reshape(KT, P) for b in
                             (L0_gnn_bv, L0_gnn_bq, L0_gnn_bk, L0_gnn_biq, L0_gnn_bik)]).T
    edge = [np.concatenate([np.asarray(a, np.int32), np.full(EC * P - E, f, np.int32)]).reshape(EC, P)
            for a, f in ((src, -1), (dst, -1), (edge_type_5, 1))]
    return {
        "x": np.asarray(x), "weights": weights, "biases": np.ascontiguousarray(biases),
        "bias_iv": np.asarray(L0_gnn_biv), "bias_o": np.asarray(L0_gnn_bo),
        "edge_cols": np.ascontiguousarray(np.stack(edge).transpose(2, 0, 1)),
        "edge_rows": np.ascontiguousarray(np.stack(edge[:2]).transpose(1, 0, 2)),
        "edge_w": np.asarray(L0_gnn_edge_type_weights),
        "clips": np.concatenate([np.asarray(L0_ffn_clip_x), np.asarray(L0_ffn_clip_down)]),
        "w_gate_up": np.concatenate([np.asarray(L0_ffn_w_gate), np.asarray(L0_ffn_w_up)]).reshape(2 * IT, IW, C),
        "w_down": np.asarray(L0_ffn_w_down).reshape(KT, P, I_F),
    }


def kernel(**inputs):
    import numpy as np
    import concourse.bacc as bacc
    from concourse.bass_utils import run_bass_kernel_spmd

    nc = bacc.Bacc("TRN2", target_bir_lowering=False, num_devices=1)
    arrays = {f"in_{k}": np.ascontiguousarray(v) for k, v in layout(**inputs).items()}
    args = [nc.dram_tensor(f"in_{n}", arrays[f"in_{n}"].shape, mybir.dt.from_np(arrays[f"in_{n}"].dtype),
                           kind="ExternalInput").ap() for n in NAMES]
    key_rows = nc.dram_tensor("key_rows", (EC, P), F32, kind="Internal").ap()
    down_scale_row = nc.dram_tensor("down_scale_row", (C,), F32, kind="Internal").ap()
    out = nc.dram_tensor("out", (N, C), F32, kind="ExternalOutput").ap()
    gnn_ffn(nc, *args, key_rows, down_scale_row, out)
    result = run_bass_kernel_spmd(nc, [arrays], core_ids=[0])
    return result.results[0]["out"]
```

```python
from contextlib import ExitStack

import concourse.bass as bass
from concourse import mybir

F32 = mybir.dt.float32
F32R = mybir.dt.float32r
BF16 = mybir.dt.bfloat16
F16 = mybir.dt.float16
I32 = mybir.dt.int32
ALU = mybir.AluOpType
ACT = mybir.ActivationFunctionType
X_AXIS = mybir.AxisListType.X
AXES = (X_AXIS, mybir.AxisListType.XY)

P = 128
N = 384
NT = N // P
C = 1024
KT = C // P
PAIRS = 8
D = 64
HC = C // 2
E = 6528
EPS = 7
EC = 8 * EPS
ONE_HOT = (7, 6)
I_F = 352
I_TILES = [(0, P), (P, P), (2 * P, I_F - 2 * P)]
IT = len(I_TILES)
RING = 4
STAGE = 2
CV, CIV, CQ, CK, CPAIR, CO = 0, 8, 16, 24, 32, 48
CHUNKS = 56
AHEAD = 2
MAGIC = 1.5 * 2.0 ** 23
NO_EDGE = -1e30
QMAX = 127.0
LN_EPS = 1e-5
SCALE = 1.0 / D ** 0.5
BIAS_V, BIAS_Q, BIAS_K, BIAS_IQ, BIAS_IK, BIAS_IV = (KT * i for i in range(6))
CODE_LOW = -108


def gnn_ffn(nc, x, weights, biases, bias_o, edge_cols, edge_rows, edge_w, clips,
            w_gate_up, w_down, key_rows, down_scale_row, out):
    with ExitStack() as ctx:
        def sb(name, shape, dt):
            return ctx.enter_context(nc.sbuf_tensor(name, shape, dt))

        def sem(name):
            return ctx.enter_context(nc.semaphore(name))

        X = sb("X", [P, NT, C], F32)
        XT = [sb(f"XT{i}", [P, KT, N], F32R) for i in range(2)]
        AT = [sb(f"AT{i}", [P, KT, N], F32R) for i in range(2)]
        QT = [sb(f"QT{i}", [P, KT, N], F32R) for i in range(2)]
        V2 = sb("V2", [P, NT, C], F32)
        stage = sb("stage", [P, STAGE, C], F32)
        ring = [sb(f"ring{i}", [P, RING, C], F32R) for i in range(2)]
        scratch = sb("scratch", [P, 3 * NT * N], F32)
        PT = [[sb(f"PT{h}{i}", [P, NT, N], F32R) for i in range(2)] for h in range(2)]
        QP = [[sb(f"QP{h}{i}", [P, N], F32R) for i in range(2)] for h in range(2)]
        KP = [sb(f"KP{i}", [P, N], F32R) for i in range(2)]
        VP = [sb(f"VP{i}", [P, NT, P], F32R) for i in range(2)]
        guT = sb("guT", [P, KT, 2 * I_F], BF16)
        wdT = sb("wdT", [P, IT, C], BF16)
        ident = sb("ident", [P, P], F32)
        wide = sb("wide", [P, 5 * P], BF16)
        tri = sb("tri", [P, P], BF16)
        iota = sb("iota", [P, N], F16)
        ones = sb("ones", [1, P], F32)
        bias = sb("bias", [P, 6 * KT], F32)
        edges = sb("edges", [P, 3, EC], I32)
        edge_row = sb("edge_row", [EC, 2, P], I32)
        key_row = sb("key_row", [EC, P], F32)
        ecol = sb("ecol", [P, 8, EC], F32)
        code_e = sb("code_e", [P, EC], I32)
        dup = sb("dup", [P, EC], F32)
        diag = sb("diag", [P, P], BF16)
        ew = sb("ew", [P, 8, 4], F32)
        clip = sb("clip", [P, 4, 2], F32)
        stats = sb("stats", [P, NT, 2, 6], F32)
        mv = sb("mv", [P, NT, 2], F32)
        rs = sb("rs", [P, 6, NT], F32)
        smx = sb("smx", [P, 4, 2 * NT], F32)
        wsc = sb("wsc", [P, 4, 2 * IT], F32)
        kinds = sb("kinds", [P, 4], F32)
        dsc = sb("dsc", [P, 4, KT], F32)
        ds_row = key_row[0:KT, :]
        gmx = sb("gmx", [P, 13], F32)
        nmean = sb("nmean", [P, NT], F32)
        PS = ctx.enter_context(nc.psum_tensor("PS", [P, 8, HC], F32))
        PROJ, TPOSE, SCORE, OUT = 0, 2, 4, 6
        ACC = 4

        key_bc = scratch[:, 0:2 * EPS * P].rearrange("p (b e j) -> p b e j", b=2, e=EPS)
        same = scratch[:, 2 * EPS * P:2 * EPS * P + EPS * P // 2].bitcast(BF16).rearrange("p (e j) -> p e j", e=EPS)
        onehot = scratch[:, 0:EPS * N].bitcast(BF16).rearrange("p (e s n) -> p e s n", e=EPS, s=2)
        gu_in = [V2[:, 0:2, HC:C], scratch[:, 0:C].rearrange("p (b c) -> p b c", b=2)]
        dn_in = [V2[:, 2, HC:HC + I_F], scratch[:, C:C + I_F]]
        at = 2 * EPS * P + EPS * P // 2
        gu_q = scratch[:, at:at + C // 2].bitcast(BF16).rearrange("p (b c) -> p b c", b=2)
        dn_q = scratch[:, at + C // 2:at + C // 2 + I_F // 2].bitcast(BF16)
        SM = [scratch[:, h * NT * N:(h + 1) * NT * N].rearrange("p (t n) -> p t n", t=NT) for h in range(2)]
        mask = scratch[:, 2 * NT * N:3 * NT * N].rearrange("p (t n) -> p t n", t=NT)
        bo_bc = guT[:, :, :].rearrange("p k i -> p (k i)")[:, 0:2 * C].bitcast(F32)
        at = KT * N // 2
        xqT = scratch[:, 0:at].bitcast(BF16).rearrange("p (k n) -> p k n", k=KT)
        hq = scratch[:, at:at + IT * N // 2].bitcast(BF16).rearrange("p (i n) -> p i n", i=IT)
        at += IT * N // 2
        xq = [area.bitcast(BF16).rearrange("p (t c) -> p t c", t=NT)
              for area in (stage[:, 1, 0:NT * HC // 2], scratch[:, at:at + NT * HC // 2])]
        ds_bc = stage[:, 0, :]
        sig, hid = V2[:, :, 0:N], V2[:, :, HC:HC + N]
        iota_i = scratch[:, 3 * C:3 * C + N].bitcast(I32)
        gu_ps = PS[:, 2, :].bitcast(BF16).rearrange("p (k i) -> p k i", k=KT)
        dn_ps = PS[:, 3, :].bitcast(BF16)[:, 0:IT * P].rearrange("p (i o) -> p i o", i=IT)

        WO, GATE, UP, DOWN, RED = (4, 0, 6), (0, 1, 2), (3, 6, 7), (0, 1, 2, 3, 6, 7), ((2, 3), (4, 5))

        def wo_chunk(c):
            if c < RING:
                return [ring[i][:, c, :] for i in range(2)]
            area, at_c = (QT, (c - RING) * C) if c < 7 else (AT, 0)
            return [area[i][:, :, :].rearrange("p k n -> p (k n)")[:, at_c:at_c + C] for i in range(2)]

        def xq_ps(b):
            return PS[:, 4 + b, :].bitcast(BF16)[:, 0:2 * N].rearrange("p (k n) -> p k n", k=2)

        stage_in = [sem(f"stage_in{i}") for i in range(STAGE)]
        w_high = sem("w_high")
        w_low = sem("w_low")
        w_used = sem("w_used")
        x_in = [sem(f"x_in{i}") for i in range(NT)]
        edges_in = sem("edges_in")
        small_in = sem("small_in")
        bc_in = sem("bc_in")
        bo_added = sem("bo_added")
        consts = sem("consts")
        dve_chain = sem("dve_chain")
        act_chain = sem("act_chain")
        var_ready = sem("var_ready")
        root_ready = sem("root_ready")
        y_ready = sem("y_ready")
        t_full = sem("t_full")
        t_high = sem("t_high")
        t_low = sem("t_low")
        proj_high = sem("proj_high")
        proj_low = sem("proj_low")
        acc_free = sem("acc_free")
        keys_made = sem("keys_made")
        keys_out = sem("keys_out")
        key_in = [sem(f"key_in{i}") for i in range(2)]
        key_used = sem("key_used")
        oh_ready = sem("oh_ready")
        oh_used = sem("oh_used")
        diag_ready = sem("diag_ready")
        code_full = sem("code_full")
        ffn_in = [sem(f"ffn_in{i}") for i in range(2)]
        ffn_q = sem("ffn_q")
        ffn_full = sem("ffn_full")
        ffn_evac = sem("ffn_evac")
        s_full = sem("s_full")
        s_seen = sem("s_seen")
        s_free = sem("s_free")
        nb_ready = sem("nb_ready")
        exp_done = sem("exp_done")
        p_ready = sem("p_ready")
        vp_high = sem("vp_high")
        vp_low = sem("vp_low")
        o_full = sem("o_full")
        o_high = sem("o_high")
        o_low = sem("o_low")
        soft_in = sem("soft_in")
        ds_turned = sem("ds_turned")
        ds_made = sem("ds_made")
        dsc_out = sem("dsc_out")
        dsbc_in = sem("dsbc_in")
        red_t = sem("red_t")
        red_m = sem("red_m")
        red_b = sem("red_b")
        wo_full = sem("wo_full")
        centred = sem("centred")
        x_scaled = sem("x_scaled")
        t_ready = sem("t_ready")
        xq_ready = sem("xq_ready")
        xqt_full = sem("xqt_full")
        xqt_evac = sem("xqt_evac")
        scales_ready = sem("scales_ready")
        gu_full = sem("gu_full")
        sig_ready = sem("sig_ready")
        h_scale = sem("h_scale")
        ht_ready = sem("ht_ready")
        hq_ready = sem("hq_ready")
        d_full = sem("d_full")
        ds_scaled = sem("ds_scaled")
        d_scaled = sem("d_scaled")
        y_out = [sem(f"y_out{i}") for i in range(2)]
        out_done = sem("out_done")

        class Chain:

            def __init__(self, eng, s):
                self.eng, self.sem, self.n = eng, s, 0

            def link(self, ins):
                ins.then_inc(self.sem, 1)
                self.n = self.n + 1

            def join(self):
                self.eng.wait_ge(self.sem, self.n)

            def step(self, ins):
                self.link(ins)
                self.join()

        block = ctx.enter_context(nc.Block())

        @block.sync
        def _(sp):
            def load(c, slot):
                sp.dma_start(stage[:, slot, :], weights[bass.ds(c, 1), :, :].rearrange("c p n -> p (c n)")
                             ).then_inc(stage_in[slot], 16)

            def load_ffn(i, j):
                slot = j % 2
                sp.wait_ge(ffn_q, 4 * i + (j + 1))
                if j < IT:
                    sp.dma_start(gu_in[slot], w_gate_up[bass.ds(IT * i + j, 1), :, :].rearrange(
                        "s p (b n) -> p (s b) n", b=2)
                                 ).then_inc(ffn_in[slot], 16)
                sp.dma_start(dn_in[slot], w_down[bass.ds(4 * i + j, 1), :, :].rearrange("s p n -> p (s n)")
                             ).then_inc(ffn_in[slot], 16)

            for t in (0, 2):
                sp.dma_start(X[:, t, :], x[t * P:(t + 1) * P, :]).then_inc(x_in[t], 16)
            for c in range(STAGE):
                load(c, c)

            def chunks(first, last):
                with sp.Fori(first // 2, last // 2) as i:
                    for j in range(2):
                        sp.wait_ge(w_low, 2 * i + (j - 1))
                        load(2 * i + j, j)

            chunks(2, 4)
            sp.wait_ge(t_full, KT)
            load_ffn(0, 0)
            sp.wait_ge(keys_made, 1)
            sp.dma_start(key_rows, key_row[:, :]).then_inc(keys_out, 16)
            sp.wait_ge(keys_out, 16)
            with sp.Fori(0, 4) as i:
                for j in range(2):
                    sp.wait_ge(key_used, 2 * i + (j + 1))
                    sp.dma_start(key_bc[:, j, :, :],
                                 key_rows[bass.ds((2 * i + j) * EPS, EPS), :].unsqueeze(0).to_broadcast([P, EPS, P])
                                 ).then_inc(key_in[j], 16)
                    sp.wait_ge(w_low, 2 * i + (j + 3))
                    load(2 * i + (j + 4), j)
            sp.wait_ge(key_used, 8 + 2)
            load_ffn(0, 1)
            with sp.Fori(0, 1) as i:
                for j in range(4):
                    sp.wait_ge(w_low, 4 * i + (j + 11))
                    load(4 * i + (j + 12), j % STAGE)
                    load_ffn(i + (j + 2) // 4, (j + 2) % 4)
            for j in range(4):
                sp.wait_ge(w_low, j + 15)
                load(j + 16, j % STAGE)
                if j < 2:
                    load_ffn(1, j + 2)
            chunks(20, 38)
            sp.wait_ge(ds_made, 1)
            sp.dma_start(down_scale_row.rearrange("(s p) -> s p", p=P), ds_row[:, :]).then_inc(dsc_out, 16)
            chunks(38, CHUNKS)
            sp.wait_ge(dsc_out, 16)
            sp.wait_ge(w_low, CHUNKS - 1)
            sp.dma_start(ds_bc, down_scale_row.rearrange("(a n) -> a n", a=1).to_broadcast([P, C])
                         ).then_inc(dsbc_in, 16)
            for m in range(NT):
                for hf in range(2):
                    cs = slice(hf * HC, (hf + 1) * HC)
                    sp.wait_ge(y_out[hf], m + 1)
                    sp.dma_start(out[m * P:(m + 1) * P, cs], X[:, m, cs]).then_inc(out_done, 16)
            sp.wait_ge(out_done, 16 * 2 * NT)

        @block.gpsimd
        def _(pool):
            pool.memset(ident[:, :], 0.0).then_inc(consts, 1)
            pool.memset(wide[:, :], 0.0).then_inc(consts, 1)
            pool.memset(tri[:, :], 1.0).then_inc(consts, 1)
            pool.memset(ones[:, :], 1.0).then_inc(consts, 1)
            for w in range(4):
                ins = pool.memset(kinds[:, w:w + 1], float(w))
            ins.then_inc(consts, 1)
            pool.wait_ge(consts, 5)
            pool.affine_select(out=ident[:, :], in_=ident[:, :], compare_op=ALU.not_equal, fill=1.0,
                               base=0, pattern=[[-1, P]], channel_multiplier=1).then_inc(consts, 1)
            pool.affine_select(out=wide[:, 2 * P:3 * P], in_=wide[:, 2 * P:3 * P], compare_op=ALU.not_equal,
                               fill=1.0, base=0, pattern=[[-1, P]], channel_multiplier=1).then_inc(consts, 1)
            pool.affine_select(out=tri[:, :], in_=tri[:, :], compare_op=ALU.is_ge,
                               fill=0.0, base=-1, pattern=[[1, P]], channel_multiplier=-1).then_inc(consts, 1)
            pool.iota(iota_i, pattern=[[1, N]], base=0, channel_multiplier=0).then_inc(consts, 1)
            pool.iota(code_e[:, :], pattern=[[4, EC]], base=CODE_LOW + 127,
                      channel_multiplier=0).then_inc(consts, 1)

            def low(c, slot):
                pool.wait_ge(w_high, c + 1)
                pool.tensor_tensor(ring[1][:, slot, :], stage[:, slot % STAGE, :],
                                   ring[0][:, slot, :].bitcast(F32), ALU.subtract).then_inc(w_low, 1)

            for c in range(CIV):
                low(c, c % RING)
                if c == 2:
                    pool.wait_ge(bc_in, 16)
                    pool.wait_ge(y_ready, NT)
                if c >= 2:
                    m, hf = (c - 2) // 2, c % 2
                    cs = slice(hf * HC, (hf + 1) * HC)
                    pool.tensor_tensor(X[:, m, cs], X[:, m, cs], bo_bc[:, cs], ALU.add).then_inc(bo_added, 1)
            with pool.Fori(0, 6) as i:
                for j in range(4):
                    low(4 * i + (CIV + j), j)
            for c in range(CPAIR, CPAIR + 6):
                low(c, c % RING)

            def spare_low(c):
                pool.wait_ge(w_high, c + 1)
                high, low_part = wo_chunk(c - CO)
                pool.tensor_tensor(low_part, stage[:, c % STAGE, :], high.bitcast(F32), ALU.subtract).then_inc(w_low, 1)

            def pair_v(u):
                pool.wait_ge(vp_high, u + 1)
                pool.tensor_tensor(VP[1][:, :, :], V2[:, :, bass.ds(u * P, P)],
                                   VP[0][:, :, :].bitcast(F32), ALU.subtract).then_inc(vp_low, 1)

            with pool.Fori(0, 3) as i:
                for b in range(2):
                    pair_v(2 * i + b)
                    low(4 * i + (38 + 2 * b), (2 + 2 * b) % RING)
                    low(4 * i + (39 + 2 * b), (3 + 2 * b) % RING)
            pair_v(6)
            low(50, 2)
            low(51, 3)
            spare_low(52)
            pair_v(7)
            for c in range(53, CHUNKS):
                spare_low(c)
            for t in range(0, 2 * NT, 2):
                pool.wait_ge(d_scaled, t + 1)
                pool.tensor_tensor(X[:, t // 2, 0:HC], X[:, t // 2, 0:HC], V2[:, t // 2, 0:HC], ALU.add
                                   ).then_inc(y_out[0], 1)

        @block.scalar
        def _(act):
            chain = Chain(act, act_chain)
            act.dma_start(X[:, 1, :], x[P:2 * P, :]).then_inc(x_in[1], 16)
            act.dma_start(edge_row[:, :, :], edge_rows).then_inc(edges_in, 16)
            act.dma_start(edges[:, :, :], edge_cols).then_inc(edges_in, 16)
            act.dma_start(bias[:, :], biases).then_inc(small_in, 16)
            act.dma_start(ew[:, 0, :], edge_w.rearrange("(a n) -> a n", a=1).to_broadcast([P, 4])
                          ).then_inc(small_in, 16)
            act.dma_start(clip[:, 0, :], clips.rearrange("(a n) -> a n", a=1).to_broadcast([P, 2])
                          ).then_inc(small_in, 16)
            act.dma_start(bo_bc, bias_o.rearrange("(a n) -> a n", a=1).to_broadcast([P, C])).then_inc(bc_in, 16)
            act.wait_ge(consts, 10)
            chain.step(act.activation(rs[:, 4, :], kinds[:, 0:NT], ACT.Sqrt))

            def high(c2, c, slot):
                act.wait_ge(stage_in[slot % STAGE], 16 * (c2 + 1))
                act.wait_ge(w_used, c + 1)
                act.activation(ring[0][:, slot, :], stage[:, slot % STAGE, :], ACT.Copy).then_inc(w_high, 1)

            def spare_high(c):
                act.wait_ge(stage_in[c % STAGE], 16 * (c // 2 + 1))
                act.wait_ge(w_used, RING + (CO if c == CHUNKS - 1 else CO - 1))
                act.activation(wo_chunk(c - CO)[0], stage[:, c % STAGE, :], ACT.Copy).then_inc(w_high, 1)

            def t_take(tau, bank, dst):
                act.wait_ge(t_full, tau + 1)
                act.activation(dst, PS[:, bank, 0:N], ACT.Copy).then_inc(t_high, 1)

            for m in range(NT):
                act.wait_ge(var_ready, m + 1)
                act.activation(rs[:, 1, m:m + 1], rs[:, 0, m:m + 1], ACT.Sqrt).then_inc(root_ready, 1)
                if m < AHEAD:
                    high(0, m, m)
            for k in range(KT):
                t_take(k, k, XT[0][:, k, :])
            def early(dst, chunk0, bias0):
                with act.Fori(0, 2) as i:
                    for j in range(4):
                        high(2 * i + ((chunk0 + AHEAD + j) // 2), 4 * i + (chunk0 + AHEAD + j), (j + AHEAD) % RING)
                        act.wait_ge(w_used, 4 * i + (RING + chunk0 + j + 1))
                        act.activation(dst[0][:, bass.ds(4 * i + j, 1), :].rearrange("p k n -> p (k n)"),
                                       PS[:, PROJ + j % 2, 0:N], ACT.Identity,
                                       bias=bias[:, bass.ds(4 * i + (bias0 + j), 1)]).then_inc(proj_high, 1)

            act.wait_ge(small_in, 3 * 16)
            early(AT, CV, BIAS_V)

            act.wait_ge(bo_added, 2 * NT)
            with act.Fori(0, 2) as i:
                for j in range(4):
                    high(2 * i + ((CIV + AHEAD + j) // 2), 4 * i + (CIV + AHEAD + j), (j + AHEAD) % RING)
                    if j == 3:
                        act.wait_ge(w_used, 4 * i + (RING + CIV + 4))
                        for m in range(NT):
                            act.activation(V2[:, m, bass.ds(i * HC, HC)], PS[:, ACC + m, :], ACT.Copy
                                           ).then_inc(acc_free, 1)
                    act.wait_ge(ffn_full, 4 * i + (j + 1))
                    if j < IT:
                        i0, iw = I_TILES[j]
                        act.activation(guT[:, :, bass.ds(I_F * i + i0, iw)], gu_ps[:, :, 0:iw], ACT.Copy)
                    for t, (_, iw) in enumerate(I_TILES):
                        ins = act.activation(wdT[0:iw, t, bass.ds(4 * P * i + j * P, P)], dn_ps[0:iw, t, :], ACT.Copy)
                    ins.then_inc(ffn_evac, 1)

            chain.step(act.activation(ew[:, 1, :], ew[:, 0, :], ACT.Abs))
            chain.step(act.activation(ew[:, 2, :], ew[:, 1, :], ACT.Exp, scale=-1.0))
            act.activation(ew[:, 3, :], ew[:, 2, :], ACT.Ln, bias=1.0).then_inc(soft_in, 1)
            act.activation(clip[:, 1, :], clip[:, 0, :], ACT.Exp, scale=-1.0).then_inc(soft_in, 1)

            early(QT, CQ, BIAS_Q)
            early(AT, CK, BIAS_K)

            def q_high(t):
                act.wait_ge(w_used, 2 * t + (RING + CPAIR + 1))
                for h in range(2):
                    r = slice(h * D, h * D + D)
                    ins = act.activation(QP[h][0][r, :], PS[r, PROJ, 0:N], ACT.Identity,
                                         bias=bias[r, bass.ds(t + BIAS_IQ, 1)])
                ins.then_inc(proj_high, 1)

            def k_high(t):
                act.wait_ge(w_used, 2 * t + (RING + CPAIR + 2))
                act.activation(KP[0][:, :], PS[:, PROJ + 1, 0:N], ACT.Identity,
                               bias=bias[:, bass.ds(t + BIAS_IK, 1)]).then_inc(proj_high, 1)

            def v_high(u):
                act.wait_ge(o_full, 2 * u + 1)
                act.activation(VP[0][:, :, :], V2[:, :, bass.ds(u * P, P)],
                               ACT.Copy).then_inc(vp_high, 1)

            def exps(p, h):
                act.wait_ge(nb_ready, 2 * p + (h + 1))
                for m in range(NT):
                    ins = act.activation(SM[h][:, m, :], SM[h][:, m, :], ACT.Exp, scale=SCALE,
                                         bias=smx[:, 1, h * NT + m:h * NT + m + 1],
                                         accum_out=smx[:, 2, h * NT + m:h * NT + m + 1])
                ins.then_inc(exp_done, 1)

            def o_take(u, h):
                r = slice(h * D, h * D + D)
                act.wait_ge(o_full, 2 * u + (h + 2))
                act.activation(XT[0][r, bass.ds(u, 1), :].rearrange("p k n -> p (k n)"), PS[r, OUT + h, 0:N],
                               ACT.Identity, bias=bias[r, bass.ds(u + BIAS_IV, 1)]).then_inc(o_high, 1)

            def probs_high(u):
                for h in range(2):
                    for m in range(NT):
                        t_take(6 * u + (8 + 3 * h + m), TPOSE + (h * NT + m) % 2, PT[h][0][:, m, :])

            high(17, 34, 2)
            q_high(0)
            high(17, 35, 3)
            k_high(0)
            exps(0, 0)
            q_high(1)
            exps(0, 1)
            high(18, 36, 0)
            high(18, 37, 1)
            k_high(1)

            def pair(u, split, project, score=True):
                v_high(u)
                probs_high(u)
                if split:
                    high(*split[0])
                o_take(u, 0)
                if score:
                    exps(u + 1, 0)
                if project:
                    q_high(u + 2)
                if score:
                    exps(u + 1, 1)
                o_take(u, 1)
                if split:
                    high(*split[1])
                if project:
                    k_high(u + 2)

            with act.Fori(0, 3) as i:
                for b in range(2):
                    pair(2 * i + b, [(2 * i + (19 + b), 4 * i + (38 + 2 * b), (2 + 2 * b) % RING),
                                     (2 * i + (19 + b), 4 * i + (39 + 2 * b), (3 + 2 * b) % RING)], True)
            pair(6, [(25, 50, 2), (25, 51, 3)], False)
            spare_high(52)
            v_high(7)
            probs_high(7)
            o_take(7, 0)
            spare_high(53)
            o_take(7, 1)
            spare_high(54)
            spare_high(55)
            chain.step(act.activation(rs[:, 4, :], kinds[:, 0:NT], ACT.Sqrt))
            for m in range(NT):
                act.wait_ge(var_ready, NT + m + 1)
                act.activation(rs[:, 1, m:m + 1], rs[:, 0, m:m + 1], ACT.Sqrt).then_inc(root_ready, 1)
                act.activation(V2[:, m, :], X[:, m, :], ACT.Identity, bias=nmean[:, m:m + 1]).then_inc(centred, 1)
            chain.step(act.activation(rs[:, 4, :], kinds[:, 0:NT], ACT.Exp))
            act.wait_ge(centred, NT)
            act.wait_ge(x_scaled, 1)
            for hf in range(2):
                for m in range(NT):
                    half = V2[:, m, hf * HC:(hf + 1) * HC]
                    act.activation(half, half, ACT.Copy, scale=rs[:, 5, m:m + 1]).then_inc(t_ready, 1)
            for k in range(KT // 2):
                act.wait_ge(xqt_full, k + 1)
                act.activation(xqT[:, 2 * k:2 * k + 2, :], xq_ps(k % 2), ACT.Copy).then_inc(xqt_evac, 1)
            act.wait_ge(scales_ready, 1)
            for i, (_, iw) in enumerate(I_TILES):
                act.wait_ge(gu_full, i + 1)
                act.activation(sig[0:iw, i, :], PS[0:iw, GATE[i], 0:N], ACT.Exp,
                               scale=wsc[0:iw, 3, i:i + 1]).then_inc(sig_ready, 1)
            act.wait_ge(h_scale, 1)
            for i, (_, iw) in enumerate(I_TILES):
                act.activation(hid[0:iw, i, :], hid[0:iw, i, :], ACT.Copy,
                               scale=gmx[0:iw, 12:13]).then_inc(ht_ready, 1)
            act.wait_ge(dsbc_in, 16)
            act.activation(ds_bc, ds_bc, ACT.Copy, scale=gmx[:, 10:11]).then_inc(ds_scaled, 1)

        @block.tensor
        def _(pe):
            pe.sem_inc(w_used, RING)
            pe.sem_inc(oh_used, EPS)
            pe.sem_inc(o_full, 1)
            pe.wait_ge(consts, 10)
            for m in range(NT):
                pe.wait_ge(y_ready, m + 1)
                for k in range(KT):
                    ins = pe.transpose(PS[:, k, m * P:(m + 1) * P], V2[:, m, k * P:(k + 1) * P], ident[:, :])
                    if m == NT - 1:
                        ins.then_inc(t_full, 1)

            def passes(outs, lhs, rhs, start, stop):
                for n, (a, b) in enumerate(((0, 0), (0, 1), (1, 0))):
                    ins = pe.matmul(outs, lhs[a], rhs[b], start=start and n == 0, stop=stop and n == 2,
                                    skip_group_check=True)
                return ins

            def begin(c, a):
                pe.wait_ge(w_low, c + 1)
                if a is not None:
                    pe.wait_ge(proj_low, a + 1)

            def part(slot, bank, src, ks, after=None, turned=False):
                w = [ring[i][:, slot, :].rearrange("p (k o) -> p k o", k=KT) for i in range(2)]
                for k in ks:
                    if turned:
                        pe.wait_ge(t_low, k + 3)
                    ins = passes(PS[:, PROJ + bank, 0:N], [w[i][:, k, :] for i in range(2)],
                                 [src[i][:, k, :] for i in range(2)], k == 0, k == KT - 1)
                    if after and k < KT - 1:
                        after(k)
                return ins

            def finish(ins):
                ins.then_inc(w_used, 1)

            def project(c, a, slot, src):
                begin(c, a)
                finish(part(slot, slot % 2, src, range(KT)))

            with pe.Fori(0, 2) as i:
                for j in range(4):
                    begin(4 * i + j, 4 * i + j)
                    pe.wait_ge(t_low, j + 3)
                    finish(part(j, j % 2, XT, range(KT), turned=j == 0))

            def ffn_turn(i, j):
                pe.wait_ge(ffn_q, 4 * i + (j + 3))
                pe.wait_ge(ffn_evac, 4 * i + (j + 1))
                if j < IT:
                    iw = I_TILES[j][1]
                    for k in range(KT):
                        pe.transpose(gu_ps[:, k, 0:iw], gu_q[0:iw, k // 4, k % 4 * P:(k % 4 + 1) * P], wide[0:iw, 2 * P:2 * P + iw])
                for t, (i0, iw) in enumerate(I_TILES):
                    ins = pe.transpose(dn_ps[0:iw, t, :], dn_q[:, i0:i0 + iw], wide[:, 2 * P:3 * P])
                ins.then_inc(ffn_full, 1)

            with pe.Fori(0, 2) as i:
                for j in range(4):
                    pe.wait_ge(w_low, 4 * i + (CIV + j + 1))
                    pe.wait_ge(proj_low, 2 * j + 4)
                    w = [ring[s][:, j, :].rearrange("p (k o) -> p k o", k=2) for s in range(2)]
                    for k2 in range(2):
                        k = 2 * j + k2
                        for m in range(NT):
                            if k == 0:
                                pe.wait_ge(acc_free, NT * i + (m + 1))
                            ins = passes(PS[:, ACC + m, :], [AT[s][:, k, m * P:(m + 1) * P] for s in range(2)],
                                         [w[s][:, k2, :] for s in range(2)], k == 0, k == KT - 1)
                    ins.then_inc(w_used, 1)
                    ffn_turn(i, j)
            pe.wait_ge(ffn_evac, 8 + 1)
            pe.transpose(PS[0:KT, TPOSE, 0:P], dsc[:, 1, :], ident[:, :]).then_inc(ds_turned, 1)

            pe.wait_ge(acc_free, 3 * NT)
            pe.wait_ge(diag_ready, 1)
            for s in range(NT):
                pe.matmul(PS[:, ACC + s, 0:N], diag[:, :], wide[:, (2 - s) * P:(5 - s) * P], start=True, stop=False,
                          skip_group_check=True)

            def edge(e, slot):
                pe.wait_ge(oh_ready, e + 1)
                for s in range(NT):
                    ins = pe.matmul(PS[:, ACC + s, 0:N], onehot[:, slot, 0, s * P:(s + 1) * P],
                                    onehot[:, slot, 1, :], start=False, stop=False, skip_group_check=True)
                ins.then_inc(oh_used, 1)

            with pe.Fori(0, 2) as i:
                for j in range(4):
                    first = 2 * sum(ONE_HOT) * i + (sum(ONE_HOT) * (j // 2) + ONE_HOT[0] * (j % 2))
                    begin(4 * i + (CQ + j), 4 * i + (8 + j))
                    finish(part(j, j % 2, XT, range(KT), lambda k: edge(first + k, k) if k < ONE_HOT[j % 2] else None))
            for s in range(NT):
                ins = pe.matmul(PS[:, ACC + s, 0:N], wide[:, 0:P], wide[:, 0:N], start=False, stop=True,
                                skip_group_check=True)
            ins.then_inc(code_full, 1)

            with pe.Fori(0, 2) as i:
                for j in range(4):
                    project(4 * i + (CK + j), 4 * i + (16 + j), j, XT)

            pe.wait_ge(proj_low, 24 + 2)

            def score(p, m):
                for h in range(2):
                    pe.wait_ge(s_free, 6 * p + (2 * m + h + 1))
                    passes(PS[:, SCORE + h, 0:N], [QP[h][s][:, m * P:(m + 1) * P] for s in range(2)],
                           [KP[s][:, :] for s in range(2)], True, True).then_inc(s_full, 1)

            def turn_probs(u, h, m):
                if m == 0:
                    pe.wait_ge(p_ready, 2 * u + (h + 1))
                pe.wait_ge(t_low, 6 * u + (8 + 3 * h + m + 1))
                for n in range(NT):
                    ins = pe.transpose(PS[:, TPOSE + (h * NT + m) % 2, n * P:(n + 1) * P],
                                       SM[h][:, n, m * P:(m + 1) * P], ident[:, :])
                ins.then_inc(t_full, 1)

            def weigh(u, h):
                pe.wait_ge(vp_low, u + 1)
                pe.wait_ge(t_low, 6 * u + (8 + 3 * h + 3 + 2))
                pe.wait_ge(o_low, 2 * u + (h + 1))
                for m in range(NT):
                    ins = passes(PS[:, OUT + h, 0:N], [VP[s][:, m, :] for s in range(2)],
                                 [PT[h][s][:, m, :] for s in range(2)], m == 0, m == NT - 1)
                ins.then_inc(o_full, 1)

            project(32, 24, 0, QT)
            project(33, 25, 1, AT)
            pe.wait_ge(proj_low, 26 + 2)
            begin(34, 26)
            score(0, 0)
            part(2, 0, QT, range(0, 4))
            score(0, 1)
            finish(part(2, 0, QT, range(4, 8)))
            score(0, 2)
            project(35, 27, 3, AT)

            def pair(u, c0, slot0, scores=True, proj=True):
                a0 = 2 * u + 28
                turn_probs(u, 0, 0)
                turn_probs(u, 0, 1)
                if proj:
                    begin(c0, a0)
                    part(slot0, 0, QT, range(0, 3))
                turn_probs(u, 0, 2)
                turn_probs(u, 1, 0)
                if proj:
                    part(slot0, 0, QT, range(3, 6))
                turn_probs(u, 1, 1)
                turn_probs(u, 1, 2)
                if proj:
                    finish(part(slot0, 0, QT, range(6, 8)))
                if scores:
                    pe.wait_ge(proj_low, a0 + 2)
                    score(u + 1, 0)
                weigh(u, 0)
                if scores:
                    score(u + 1, 1)
                if proj:
                    begin(c0 + 1, a0 + 1)
                    part(slot0 + 1, 1, AT, range(0, 3))
                if scores:
                    score(u + 1, 2)
                if proj:
                    part(slot0 + 1, 1, AT, range(3, 6))
                weigh(u, 1)
                if proj:
                    finish(part(slot0 + 1, 1, AT, range(6, 8)))

            with pe.Fori(0, 3) as i:
                for b in range(2):
                    pair(2 * i + b, 4 * i + (36 + 2 * b), 2 * b)
            pair(6, None, None, True, False)
            pair(7, None, None, False, False)

            for m in range(NT):
                for hf in range(2):
                    for j in range(4):
                        if m == 0:
                            pe.wait_ge(w_low, CO + 4 * hf + j + 1)
                        if m == 0 and hf == 0:
                            pe.wait_ge(o_low, 4 * (j + 1) + 2)
                        w = [chunk[:, :].rearrange("p (k o) -> p k o", k=2) for chunk in wo_chunk(4 * hf + j)]
                        for k2 in range(2):
                            k = 2 * j + k2
                            ins = passes(PS[:, WO[m] + hf, :], [XT[i][:, k, m * P:(m + 1) * P] for i in range(2)],
                                         [w[i][:, k2, :] for i in range(2)], k == 0, k == KT - 1)
                    ins.then_inc(wo_full, 1)

            def reduce_max(n):
                row, all_rows = RED[n]
                for i in range(3):
                    pe.wait_ge(red_t, 3 * n + i + 1)
                    ins = pe.transpose(PS[0:1, row, i * P:(i + 1) * P], gmx[:, 4 * n + i:4 * n + i + 1], ident[:, :])
                ins.then_inc(red_b, 1)
                pe.wait_ge(red_m, n + 1)
                pe.matmul(PS[:, all_rows, 0:1], ones[:, :], gmx[0:1, 8:9], start=True, stop=True).then_inc(red_b, 1)

            reduce_max(0)

            def turn_ints(k):
                pe.wait_ge(xq_ready, k // 2 * NT + NT)
                if k >= 2:
                    pe.wait_ge(xqt_evac, k - 1)
                for k2 in range(2):
                    for m in range(NT):
                        cs = slice((k % 2 * 2 + k2) * P, (k % 2 * 2 + k2 + 1) * P)
                        ins = pe.transpose(xq_ps(k % 2)[:, k2, m * P:(m + 1) * P], xq[k // 2][:, m, cs],
                                           wide[:, 2 * P:3 * P])
                ins.then_inc(xqt_full, 1)

            for hf in range(2):
                turn_ints(2 * hf)
                turn_ints(2 * hf + 1)
                pe.wait_ge(xqt_evac, 2 * hf + 2)
                for g in range(2):
                    for i, (i0, iw) in enumerate(I_TILES):
                        for k in range(4 * hf, 4 * hf + 4):
                            ins = pe.matmul(PS[0:iw, (GATE, UP)[g][i], 0:N], guT[:, k, g * I_F + i0:g * I_F + i0 + iw],
                                            xqT[:, k, :], start=(k == 0), stop=(k == KT - 1), skip_group_check=True)
                        if hf == 1:
                            ins.then_inc(gu_full, 1)
            reduce_max(1)
            for t in range(2 * NT):
                m, hf = t // 2, t % 2
                for i, (_, iw) in enumerate(I_TILES):
                    if t == 0:
                        pe.wait_ge(hq_ready, i + 1)
                    ins = pe.matmul(PS[:, DOWN[t], :], hq[0:iw, i, m * P:(m + 1) * P],
                                    wdT[0:iw, i, hf * HC:(hf + 1) * HC], start=(i == 0), stop=(i == IT - 1))
                ins.then_inc(d_full, 1)

        @block.vector
        def _(dve):
            chain = Chain(dve, dve_chain)
            dve.sem_inc(t_low, 2)
            dve.sem_inc(proj_low, 2)
            dve.sem_inc(acc_free, NT)
            dve.sem_inc(key_used, 2)
            dve.sem_inc(ffn_q, 2)
            dve.sem_inc(ffn_evac, 1)
            dve.sem_inc(s_free, 2)
            dve.sem_inc(o_low, 2)
            def moments(m):
                for g in range(2):
                    chain.link(dve.bn_stats(stats[:, m, g, :], X[:, m, g * HC:(g + 1) * HC]))
                chain.join()
                chain.step(dve.bn_aggr(mv[:, m, :], stats[:, m, :, :].rearrange("p a b -> p (a b)")))
                dve.tensor_scalar(rs[:, 0, m:m + 1], mv[:, m, 1:2], LN_EPS, None, ALU.add).then_inc(var_ready, 1)

            def norm(n, m):
                v, root, inv, two = (rs[:, c, m:m + 1] for c in range(4))
                dve.wait_ge(root_ready, NT * n + m + 1)
                chain.step(dve.reciprocal(inv, root))
                chain.step(dve.scalar_tensor_tensor(two, inv, v, root, ALU.mult, ALU.add))
                chain.step(dve.tensor_scalar(two, two, 0.5, None, ALU.mult))
                chain.step(dve.reciprocal(inv, two))
                dve.tensor_scalar(V2[:, m, :], X[:, m, :], mv[:, m, 0:1], inv,
                                  ALU.subtract, ALU.mult).then_inc(y_ready, 1)

            for m in range(NT):
                dve.wait_ge(x_in[m], 16)
                moments(m)
                if m:
                    norm(0, m - 1)
            norm(0, NT - 1)
            dve.wait_ge(edges_in, 2 * 16)
            dve.scalar_tensor_tensor(key_row[:, :], edge_row[:, 0, :], float(N), edge_row[:, 1, :],
                                     ALU.mult, ALU.add).then_inc(keys_made, 1)

            def t_rest(tau, bank, high, low):
                dve.wait_ge(t_high, tau + 1)
                dve.tensor_tensor(low, PS[:, bank, 0:N], high.bitcast(F32), ALU.subtract).then_inc(t_low, 1)

            for k in range(KT):
                t_rest(k, k, XT[0][:, k, :], XT[1][:, k, :])
            SRC, DST, KEY, TYP, NEG, VAL = range(6)
            chain.link(dve.tensor_copy(ecol[:, SRC, :], edges[:, 0, :]))
            chain.link(dve.tensor_copy(ecol[:, DST, :], edges[:, 1, :]))
            chain.step(dve.tensor_scalar(ecol[:, TYP, :], edges[:, 2, :], 4.0, -1.0, ALU.min, ALU.add))
            chain.link(dve.scalar_tensor_tensor(ecol[:, KEY, :], ecol[:, SRC, :], float(N), ecol[:, DST, :],
                                                ALU.mult, ALU.add))
            chain.step(dve.tensor_scalar(ecol[:, NEG, :], ecol[:, TYP, :], 0.0, 4.0, ALU.is_lt, ALU.mult))
            chain.step(dve.tensor_tensor(ecol[:, TYP, :], ecol[:, TYP, :], ecol[:, NEG, :], ALU.add))
            chain.step(dve.tensor_scalar(ecol[:, TYP, :], ecol[:, TYP, :], 0.25, 1.0, ALU.mult, ALU.add))
            dve.wait_ge(consts, 10)
            chain.step(dve.tensor_scalar(code_e[:, :], code_e[:, :], 23, None, ALU.logical_shift_left))
            chain.link(dve.tensor_tensor(ecol[:, VAL, :], ecol[:, TYP, :], code_e[:, :].bitcast(F32), ALU.mult))
            chain.link(dve.tensor_copy(iota[:, :], iota_i))
            chain.link(dve.memset(gmx[:, 4:4 + IT], 0.0))
            dve.tensor_scalar(diag[:, :], ident[:, :], 1.75 * 2.0 ** (CODE_LOW - 4), None,
                              ALU.mult).then_inc(diag_ready, 1)

            for h in range(2):
                r = slice((1 - h) * D, (1 - h) * D + D)
                for s in range(2):
                    chain.link(dve.memset(QP[h][s][r, :].bitcast(F32), 0.0))

            def tile_low(a, k, b, dst, col):
                dve.wait_ge(proj_high, a + 1)
                at_k = [dst[s][:, bass.ds(k, 1), :].rearrange("p k n -> p (k n)") for s in range(2)]
                dve.scalar_tensor_tensor(at_k[1], PS[:, PROJ + b, 0:N], bias[:, bass.ds(col, 1)],
                                         at_k[0].bitcast(F32), ALU.add, ALU.subtract).then_inc(proj_low, 1)

            dve.wait_ge(small_in, 3 * 16)
            def to_ints(both, turned):
                for src, _, sc, col in both:
                    chain.link(dve.tensor_reduce(sc[:, 0, col], src, AXES[len(src.shape) - 2], ALU.max, apply_absolute_value=True))
                chain.join()
                for _, _, sc, col in both:
                    chain.link(dve.tensor_scalar(sc[:, 1, col], sc[:, 0, col], 1.0 / QMAX, None, ALU.mult))
                chain.join()
                for _, _, sc, col in both:
                    chain.link(dve.reciprocal(sc[:, 2, col], sc[:, 1, col]))
                chain.join()
                for src, _, sc, col in both:
                    chain.link(dve.tensor_scalar(src, src, sc[:, 2, col], MAGIC, ALU.mult, ALU.add))
                chain.join()
                dve.wait_ge(ffn_evac, turned)
                for src, q, _, _ in both:
                    ins = dve.tensor_scalar(q, src, MAGIC, None, ALU.subtract)
                ins.then_inc(ffn_q, 1)

            def later_edge(s, b, n):
                dve.wait_ge(key_in[b], n)
                cols = bass.ds(s * EPS, EPS) if not isinstance(s, int) else slice(s * EPS, (s + 1) * EPS)
                dve.wait_ge(key_used, s + 2)
                chain.step(dve.tensor_tensor(same[:, :, :], key_bc[:, b, :, :],
                                             ecol[:, KEY, cols].unsqueeze(2).to_broadcast([P, EPS, P]),
                                             ALU.is_equal))
                chain.step(dve.tensor_tensor(same[:, :, :], same[:, :, :],
                                             tri[:, :].unsqueeze(1).to_broadcast([P, EPS, P]), ALU.mult))
                dve.tensor_reduce(dup[:, cols], same[:, :, :], X_AXIS, ALU.max).then_inc(key_used, 1)

            def ffn_step(i, j):
                dve.wait_ge(ffn_in[j % 2], [64 * i + 32, 48 * i + 32, 64 * i + 64, 48 * i + 48][j])
                gu = [(gu_in[j % 2], gu_q, wsc, bass.ds(IT * i + j, 1))] if j < IT else []
                to_ints(gu + [(dn_in[j % 2], dn_q, dsc, bass.ds(4 * i + j, 1))], 4 * i + (j + 1))

            base = chain.n
            with dve.Fori(0, 3) as i:
                for b in range(2):
                    chain.n = 4 * i + (base + 2 * b)
                    later_edge(2 * i + b, b, 16 * i + 16)
                    tile_low(2 * i + b, 2 * i + b, b, AT, 2 * i + (BIAS_V + b))
            chain.n = base + 12
            later_edge(6, 0, 4 * 16)
            tile_low(6, 6, 0, AT, BIAS_V + 6)
            ffn_step(0, 0)
            tile_low(7, 7, 1, AT, BIAS_V + 7)
            later_edge(7, 1, 4 * 16)
            dve.wait_ge(key_used, 8 + 2)
            chain.step(dve.tensor_scalar(dup[:, :], dup[:, :], -1.0, 1.0, ALU.mult, ALU.add))
            chain.step(dve.tensor_tensor(ecol[:, VAL, :], ecol[:, VAL, :], dup[:, :], ALU.mult))

            for s in range(1, 8):
                ffn_step(s // 4, s % 4)
            dve.wait_ge(ds_turned, 1)
            dve.tensor_copy(ds_row[:, :], PS[0:KT, TPOSE, 0:P]).then_inc(ds_made, 1)


            dve.wait_ge(ffn_full, 8)

            def one_hot(first, before, n):
                for s in range(n):
                    e = first + s
                    dve.wait_ge(oh_used, before + (min(s, ONE_HOT[1] - 1) + 1 + EPS))
                    dve.tensor_scalar(onehot[:, s, 0, :], iota[:, :], ecol[:, SRC, bass.ds(e, 1)],
                                      ecol[:, VAL, bass.ds(e, 1)], ALU.is_equal, ALU.mult)
                    dve.tensor_scalar(onehot[:, s, 1, :], iota[:, :], ecol[:, DST, bass.ds(e, 1)],
                                      None, ALU.is_equal).then_inc(oh_ready, 1)

            def q_tile(s, b):
                tile_low(s + 8, s, b, QT, s + BIAS_Q)

            ROUND = sum(ONE_HOT)
            one_hot(0, -EPS, ONE_HOT[0])
            with dve.Fori(0, 3) as i:
                one_hot(ROUND * i + ONE_HOT[0], ROUND * i, ONE_HOT[1])
                q_tile(2 * i, 0)
                one_hot(ROUND * i + ROUND, ROUND * i + ONE_HOT[0], ONE_HOT[0])
                q_tile(2 * i + 1, 1)
            one_hot(3 * ROUND + ONE_HOT[0], 3 * ROUND, ONE_HOT[1])
            q_tile(6, 0)
            q_tile(7, 1)
            dve.wait_ge(soft_in, 2)
            chain.step(dve.scalar_tensor_tensor(ew[:, 4, :], ew[:, 0, :], 0.0, ew[:, 3, :], ALU.max, ALU.add))
            chain.step(dve.tensor_scalar(ew[:, 5, :], ew[:, 4, :], 1.0 / SCALE, None, ALU.mult))
            chain.step(dve.tensor_scalar(clip[:, 2, :], clip[:, 1, :], 1.0, None, ALU.add))
            chain.step(dve.reciprocal(clip[:, 3, :], clip[:, 2, :]))
            chain.step(dve.tensor_scalar(clip[:, 2, :], clip[:, 3, :], 1.0 / QMAX, None, ALU.mult))
            code = PS[:, ACC:ACC + NT, 0:N]
            dve.wait_ge(code_full, 1)
            kind = SM[0].bitcast(I32)
            chain.step(dve.tensor_scalar(kind, code.bitcast(I32), 21, 3, ALU.logical_shift_right, ALU.bitwise_and))
            chain.step(dve.tensor_scalar(mask, code, 0.0, NO_EDGE, ALU.is_equal, ALU.mult))
            base = chain.n
            with dve.Fori(0, 4) as w:
                chain.n = 2 * w + base
                tile_low(2 * w + 16, 2 * w, 0, AT, 2 * w + BIAS_K)
                chain.step(dve.tensor_scalar(SM[1], kind, kinds[:, bass.ds(w, 1)], ew[:, 5, bass.ds(w, 1)],
                                             ALU.is_equal, ALU.mult))
                tile_low(2 * w + 17, 2 * w + 1, 1, AT, 2 * w + (BIAS_K + 1))
                chain.step(dve.tensor_tensor(mask, mask, SM[1], ALU.add))
            chain.n = base + 8

            def q_low(t):
                dve.wait_ge(proj_high, 2 * t + 25)
                for h in range(2):
                    r = slice(h * D, h * D + D)
                    ins = dve.scalar_tensor_tensor(QP[h][1][r, :], PS[r, PROJ, 0:N], bias[r, bass.ds(t + BIAS_IQ, 1)],
                                                   QP[h][0][r, :].bitcast(F32), ALU.add, ALU.subtract)
                ins.then_inc(proj_low, 1)

            def k_low(t):
                dve.wait_ge(proj_high, 2 * t + 26)
                dve.scalar_tensor_tensor(KP[1][:, :], PS[:, PROJ + 1, 0:N], bias[:, bass.ds(t + BIAS_IK, 1)],
                                         KP[0][:, :].bitcast(F32), ALU.add, ALU.subtract).then_inc(proj_low, 1)

            def masked(p, m):
                for h in range(2):
                    dve.wait_ge(s_full, 6 * p + (2 * m + h + 1))
                    dve.sem_inc(s_seen, 1)
                    dve.tensor_tensor_reduce(SM[h][:, m, :], PS[:, SCORE + h, 0:N], mask[:, m, :], 1.0, -3e38,
                                             ALU.add, ALU.max, smx[:, 0, h * NT + m:h * NT + m + 1]
                                             ).then_inc(s_free, 1)

            def negate(p):
                dve.wait_ge(s_free, 6 * p + (6 + 2))
                for h in range(2):
                    hs = slice(h * NT, (h + 1) * NT)
                    dve.tensor_scalar(smx[:, 1, hs], smx[:, 0, hs], -SCALE, None, ALU.mult).then_inc(nb_ready, 1)

            def normalise(p, h):
                hs = slice(h * NT, (h + 1) * NT)
                dve.wait_ge(exp_done, 2 * p + (h + 1))
                chain.step(dve.reciprocal(smx[:, 3, hs], smx[:, 2, hs]))
                for m in range(NT):
                    ins = dve.tensor_scalar(SM[h][:, m, :], SM[h][:, m, :], smx[:, 3, h * NT + m:h * NT + m + 1],
                                            None, ALU.mult)
                ins.then_inc(p_ready, 1)

            def o_rest(u, h):
                r = slice(h * D, h * D + D)
                at_u = [XT[s][r, bass.ds(u, 1), :].rearrange("p k n -> p (k n)") for s in range(2)]
                dve.wait_ge(o_high, 2 * u + (h + 1))
                dve.scalar_tensor_tensor(at_u[1], PS[r, OUT + h, 0:N], bias[r, bass.ds(u + BIAS_IV, 1)],
                                         at_u[0].bitcast(F32), ALU.add, ALU.subtract).then_inc(o_low, 1)

            q_low(0)
            k_low(0)
            masked(0, 0)
            masked(0, 1)
            masked(0, 2)
            negate(0)
            q_low(1)
            normalise(0, 0)
            normalise(0, 1)
            k_low(1)

            def pair(u, scores=True, proj=True):
                for h in range(2):
                    for m in range(NT):
                        t_rest(6 * u + (8 + 3 * h + m), TPOSE + (h * NT + m) % 2, PT[h][0][:, m, :], PT[h][1][:, m, :])
                if scores:
                    masked(u + 1, 0)
                    masked(u + 1, 1)
                    masked(u + 1, 2)
                    negate(u + 1)
                o_rest(u, 0)
                if proj:
                    q_low(u + 2)
                if scores:
                    normalise(u + 1, 0)
                    normalise(u + 1, 1)
                o_rest(u, 1)
                if proj:
                    k_low(u + 2)

            base = chain.n
            with dve.Fori(0, 3) as i:
                for b in range(2):
                    chain.n = 4 * i + (base + 2 * b)
                    pair(2 * i + b)
            chain.n = base + 12
            pair(6, True, False)
            pair(7, False, False)

            def greatest(n):
                row, all_rows = RED[n]
                dve.wait_ge(red_b, 2 * n + 1)
                dve.tensor_reduce(gmx[0:1, 8:9], PS[0:1, row, 0:3 * P], X_AXIS, ALU.max).then_inc(red_m, 1)
                dve.wait_ge(red_b, 2 * n + 2)
                chain.step(dve.tensor_tensor(gmx[:, 9 + n:10 + n], PS[:, all_rows, 0:1], clip[:, 2, n:n + 1], ALU.mult))

            most, least, over, under = (smx[:, c, :] for c in range(4))
            for m in range(NT):
                mean, inv = mv[:, m, 0:1], rs[:, 2, m:m + 1]
                for hf in range(2):
                    t = 2 * m + hf
                    cs = slice(hf * HC, (hf + 1) * HC)
                    dve.wait_ge(wo_full, t + 1)
                    dve.sem_inc(s_seen, 1)
                    chain.step(dve.tensor_tensor_reduce(X[:, m, cs], PS[:, WO[m] + hf, :], X[:, m, cs], 1.0, -3e38,
                                                        ALU.add, ALU.max, most[:, t:t + 1]))
                    chain.link(dve.bn_stats(stats[:, m, hf, :], X[:, m, cs]))
                    if t < 2 * NT - 1:
                        chain.link(dve.tensor_reduce(least[:, t:t + 1], X[:, m, cs], X_AXIS, ALU.min))
                chain.join()
                chain.step(dve.bn_aggr(mv[:, m, :], stats[:, m, :, :].rearrange("p a b -> p (a b)")))
                dve.tensor_scalar(nmean[:, m:m + 1], mean, -1.0, None, ALU.mult)
                dve.tensor_scalar(rs[:, 0, m:m + 1], mv[:, m, 1:2], LN_EPS, None, ALU.add).then_inc(var_ready, 1)
                if m == NT - 1:
                    chain.step(dve.tensor_reduce(least[:, t:t + 1], X[:, m, cs], X_AXIS, ALU.min))
                t = 2 * m
                chain.link(dve.tensor_scalar(over[:, m:m + 1], most[:, t:t + 1], most[:, t + 1:t + 2], mean,
                                             ALU.max, ALU.subtract))
                chain.link(dve.tensor_scalar(under[:, m:m + 1], least[:, t:t + 1], least[:, t + 1:t + 2], mean,
                                             ALU.min, ALU.subtract))
                dve.wait_ge(root_ready, NT + m + 1)
                chain.step(dve.reciprocal(inv, rs[:, 1, m:m + 1]))
                chain.link(dve.scalar_tensor_tensor(over[:, m:m + 1], under[:, m:m + 1], -1.0, over[:, m:m + 1],
                                                    ALU.mult, ALU.max))
                chain.step(dve.scalar_tensor_tensor(rs[:, 3, m:m + 1], inv, rs[:, 0, m:m + 1], rs[:, 1, m:m + 1],
                                                    ALU.mult, ALU.add))
                chain.step(dve.reciprocal(inv, rs[:, 3, m:m + 1]))
                dve.tensor_tensor(gmx[:, m:m + 1], over[:, m:m + 1], inv, ALU.mult).then_inc(red_t, 1)

            greatest(0)
            chain.step(dve.reciprocal(gmx[:, 11:12], gmx[:, 9:10]))
            dve.tensor_scalar(rs[:, 5, :], rs[:, 2, :], gmx[:, 11:12], None, ALU.mult).then_inc(x_scaled, 1)
            chain.step(dve.tensor_scalar(wsc[:, 2, :], wsc[:, 1, :], gmx[:, 9:10], 2.0, ALU.mult, ALU.mult))
            dve.tensor_scalar(wsc[:, 3, :], wsc[:, 2, :], -1.0, None, ALU.mult).then_inc(scales_ready, 1)

            def round_off(src, dst):
                chain.step(dve.tensor_scalar(src, src, QMAX, -QMAX - 1.0, ALU.min, ALU.max))
                return dve.tensor_scalar(dst, src, MAGIC, MAGIC, ALU.add, ALU.subtract)

            for hf in range(2):
                for m in range(NT):
                    dve.wait_ge(t_ready, NT * hf + m + 1)
                    round_off(V2[:, m, hf * HC:(hf + 1) * HC], xq[hf][:, m, :]).then_inc(xq_ready, 1)
            for i, (_, iw) in enumerate(I_TILES):
                sg, ht = sig[0:iw, i, :], hid[0:iw, i, :]
                dve.wait_ge(sig_ready, i + 1)
                chain.step(dve.tensor_scalar(sg, sg, 1.0, None, ALU.add))
                chain.step(dve.reciprocal(sg, sg))
                chain.link(dve.scalar_tensor_tensor(ht, PS[0:iw, GATE[i], 0:N], wsc[0:iw, 2, i:i + 1], sg,
                                                    ALU.mult, ALU.mult))
            chain.join()
            for i, (_, iw) in enumerate(I_TILES):
                ht = hid[0:iw, i, :]
                dve.wait_ge(gu_full, IT + i + 1)
                chain.step(dve.scalar_tensor_tensor(ht, PS[0:iw, UP[i], 0:N], wsc[0:iw, 2, IT + i:IT + i + 1], ht,
                                                    ALU.mult, ALU.mult))
                dve.tensor_reduce(gmx[0:iw, 4 + i:5 + i], ht, X_AXIS, ALU.max, apply_absolute_value=True
                                  ).then_inc(red_t, 1)
            greatest(1)
            dve.reciprocal(gmx[:, 12:13], gmx[:, 10:11]).then_inc(h_scale, 1)
            for i, (_, iw) in enumerate(I_TILES):
                dve.wait_ge(ht_ready, i + 1)
                round_off(hid[0:iw, i, :], hq[0:iw, i, :]).then_inc(hq_ready, 1)
            dve.wait_ge(hq_ready, IT)
            dve.wait_ge(ds_scaled, 1)
            for t in range(2 * NT):
                m, cs = t // 2, slice(t % 2 * HC, (t % 2 + 1) * HC)
                dve.wait_ge(d_full, t + 1)
                dve.tensor_tensor(V2[:, m, cs], PS[:, DOWN[t], :], ds_bc[:, cs], ALU.mult).then_inc(d_scaled, 1)
                if t % 2:
                    dve.wait_ge(d_scaled, t + 1)
                    dve.tensor_tensor(X[:, m, cs], X[:, m, cs], V2[:, m, cs], ALU.add).then_inc(y_out[1], 1)


NAMES = ["x", "weights", "biases", "bias_o", "edge_cols", "edge_rows", "edge_w", "clips",
         "w_gate_up", "w_down"]


def layout(x, src, dst, edge_type_5, L0_gnn_edge_type_weights, L0_gnn_wq, L0_gnn_bq, L0_gnn_wk, L0_gnn_bk,
           L0_gnn_wv, L0_gnn_bv, L0_gnn_wiq, L0_gnn_biq, L0_gnn_wik, L0_gnn_bik, L0_gnn_wiv, L0_gnn_biv,
           L0_gnn_wo, L0_gnn_bo, L0_ffn_clip_x, L0_ffn_clip_down, L0_ffn_w_gate, L0_ffn_w_up, L0_ffn_w_down):
    import numpy as np

    def tiles(w):
        return np.asarray(w).reshape(KT, P, KT, P).transpose(0, 3, 2, 1).reshape(KT, P, C)

    def halves(w):
        return np.asarray(w).reshape(2, HC, 4, 2, P).transpose(0, 2, 4, 3, 1).reshape(8, P, C)

    pairs = np.stack([tiles(L0_gnn_wiq), tiles(L0_gnn_wik)], axis=1).reshape(16, P, C)
    weights = np.concatenate([tiles(L0_gnn_wv), halves(L0_gnn_wiv), tiles(L0_gnn_wq), tiles(L0_gnn_wk), pairs,
                              halves(L0_gnn_wo)])
    biases = np.concatenate([np.asarray(b).reshape(KT, P) for b in
                             (L0_gnn_bv, L0_gnn_bq, L0_gnn_bk, L0_gnn_biq, L0_gnn_bik, L0_gnn_biv)]).T
    ones = np.ones((IT * P - I_F, C), np.float32)
    edge = [np.concatenate([np.asarray(a, np.int32), np.full(EC * P - E, f, np.int32)]).reshape(EC, P)
            for a, f in ((src, -1), (dst, -1), (edge_type_5, 1))]
    return {
        "x": np.asarray(x), "weights": weights, "biases": np.ascontiguousarray(biases),
        "bias_o": np.asarray(L0_gnn_bo),
        "edge_cols": np.ascontiguousarray(np.stack(edge).transpose(2, 0, 1)),
        "edge_rows": np.ascontiguousarray(np.stack(edge[:2]).transpose(1, 0, 2)),
        "edge_w": np.asarray(L0_gnn_edge_type_weights),
        "clips": np.concatenate([np.asarray(L0_ffn_clip_x), np.asarray(L0_ffn_clip_down)]),
        "w_gate_up": np.concatenate([np.asarray(L0_ffn_w_gate), ones, np.asarray(L0_ffn_w_up), ones]
                                    ).reshape(2 * IT, P, C),
        "w_down": np.asarray(L0_ffn_w_down).reshape(KT, P, I_F),
    }


def kernel(**inputs):
    import numpy as np
    import concourse.bacc as bacc
    from concourse.bass_utils import run_bass_kernel_spmd

    nc = bacc.Bacc("TRN2", target_bir_lowering=False, num_devices=1)
    arrays = {f"in_{k}": np.ascontiguousarray(v) for k, v in layout(**inputs).items()}
    args = [nc.dram_tensor(f"in_{n}", arrays[f"in_{n}"].shape, mybir.dt.from_np(arrays[f"in_{n}"].dtype),
                           kind="ExternalInput").ap() for n in NAMES]
    key_rows = nc.dram_tensor("key_rows", (EC, P), F32, kind="Internal").ap()
    down_scale_row = nc.dram_tensor("down_scale_row", (C,), F32, kind="Internal").ap()
    out = nc.dram_tensor("out", (N, C), F32, kind="ExternalOutput").ap()
    gnn_ffn(nc, *args, key_rows, down_scale_row, out)
    result = run_bass_kernel_spmd(nc, [arrays], core_ids=[0])
    return result.results[0]["out"]
```

```python
from contextlib import ExitStack

import concourse.bass as bass
from concourse import mybir

F32 = mybir.dt.float32
F32R = mybir.dt.float32r
BF16 = mybir.dt.bfloat16
F16 = mybir.dt.float16
I32 = mybir.dt.int32
ALU = mybir.AluOpType
ACT = mybir.ActivationFunctionType
X_AXIS = mybir.AxisListType.X
AXES = (X_AXIS, mybir.AxisListType.XY)

P = 128
N = 384
NT = N // P
C = 1024
KT = C // P
D = 64
HC = C // 2
E = 6528
EPS = 7
EC = 8 * EPS
ONE_HOT = (7, 6)
I_F = 352
I_TILES = [(0, P), (P, P), (2 * P, I_F - 2 * P)]
IT = len(I_TILES)
RING = 4
STAGE = 2
CV, CIV, CQ, CK, CPAIR, CO = 0, 8, 16, 24, 32, 48
CHUNKS = 56
AHEAD = 2
MAGIC = 1.5 * 2.0 ** 23
NO_EDGE = -1e30
QMAX = 127.0
LN_EPS = 1e-5
SCALE = 1.0 / D ** 0.5
BIAS_V, BIAS_Q, BIAS_K, BIAS_IQ, BIAS_IK, BIAS_IV = (KT * i for i in range(6))
CODE_LOW = -108


def gnn_ffn(nc, x, weights, biases, bias_o, edge_cols, edge_rows, edge_w, clips,
            w_gate_up, w_down, key_rows, down_scale_row, out):
    with ExitStack() as ctx:
        def sb(name, shape, dt):
            return ctx.enter_context(nc.sbuf_tensor(name, shape, dt))

        def sem(name):
            return ctx.enter_context(nc.semaphore(name))

        X = sb("X", [P, NT, C], F32)
        XT = [sb(f"XT{i}", [P, KT, N], F32R) for i in range(2)]
        AT = [sb(f"AT{i}", [P, KT, N], F32R) for i in range(2)]
        QT = [sb(f"QT{i}", [P, KT, N], F32R) for i in range(2)]
        V2 = sb("V2", [P, NT, C], F32)
        stage = sb("stage", [P, STAGE, C], F32)
        ring = [sb(f"ring{i}", [P, RING, C], F32R) for i in range(2)]
        scratch = sb("scratch", [P, 3 * NT * N], F32)
        PT = [[sb(f"PT{h}{i}", [P, NT, N], F32R) for i in range(2)] for h in range(2)]
        QP = [sb(f"QP{h}", [P, N], F32R) for h in range(2)]
        KH = [sb(f"KH{h}", [P, N], F32R) for h in range(2)]
        KL = [sb(f"KL{h}", [P, N], F32R) for h in range(2)]
        ROWS = [slice(h * D, h * D + D) for h in range(2)]
        VP = [sb(f"VP{i}", [P, NT, P], F32R) for i in range(2)]
        guT = sb("guT", [P, KT, 2 * I_F], BF16)
        wdT = sb("wdT", [P, IT, C], BF16)
        ident = sb("ident", [P, P], F32)
        wide = sb("wide", [P, 5 * P], BF16)
        tri = sb("tri", [P, P], BF16)
        iota = sb("iota", [P, N], F16)
        ones = sb("ones", [1, P], F32)
        bias = sb("bias", [P, 6 * KT], F32)
        edges = sb("edges", [P, 3, EC], I32)
        edge_row = sb("edge_row", [EC, 2, P], I32)
        key_row = sb("key_row", [EC, P], F32)
        ecol = sb("ecol", [P, 8, EC], F32)
        code_e = sb("code_e", [P, EC], I32)
        dup = sb("dup", [P, EC], F32)
        diag = sb("diag", [P, P], BF16)
        ew = sb("ew", [P, 8, 4], F32)
        clip = sb("clip", [P, 4, 2], F32)
        stats = sb("stats", [P, NT, 2, 6], F32)
        mv = sb("mv", [P, NT, 2], F32)
        rs = sb("rs", [P, 6, NT], F32)
        smx = sb("smx", [P, 4, 2 * NT], F32)
        wsc = sb("wsc", [P, 3, 2 * IT], F32)
        kinds = sb("kinds", [P, 4], F32)
        dsc = sb("dsc", [P, 4, KT], F32)
        ds_row = key_row[0:KT, :]
        gmx = sb("gmx", [P, 13], F32)
        nmean = sb("nmean", [P, NT], F32)
        PS = ctx.enter_context(nc.psum_tensor("PS", [P, 8, HC], F32))
        PROJ, TPOSE, SCORE, OUT = 0, 2, 4, 6
        ACC = 4
        INNER_V = (7, 6, 0)

        key_bc = scratch[:, 0:2 * EPS * P].rearrange("p (b e j) -> p b e j", b=2, e=EPS)
        same = scratch[:, 2 * EPS * P:2 * EPS * P + EPS * P // 2].bitcast(BF16).rearrange("p (e j) -> p e j", e=EPS)
        onehot = scratch[:, 0:EPS * N].bitcast(BF16).rearrange("p (e s n) -> p e s n", e=EPS, s=2)
        gu_in = [V2[:, 0:2, HC:C], scratch[:, 0:C].rearrange("p (b c) -> p b c", b=2), V2[:, 0:2, 0:HC]]
        dn_in = [V2[:, 2, HC:HC + I_F], scratch[:, C:C + I_F], V2[:, 2, 0:I_F]]
        at = 2 * EPS * P + EPS * P // 2
        gu_q = scratch[:, at:at + C // 2].bitcast(BF16).rearrange("p (b c) -> p b c", b=2)
        dn_q = scratch[:, at + C // 2:at + C // 2 + I_F // 2].bitcast(BF16)
        SM = [scratch[:, h * NT * N:(h + 1) * NT * N].rearrange("p (t n) -> p t n", t=NT) for h in range(2)]
        mask = scratch[:, 2 * NT * N:3 * NT * N].rearrange("p (t n) -> p t n", t=NT)
        bo_bc = guT[:, :, :].rearrange("p k i -> p (k i)")[:, 0:2 * C].bitcast(F32)
        at = KT * N // 2
        xqT = scratch[:, 0:at].bitcast(BF16).rearrange("p (k n) -> p k n", k=KT)
        hq = scratch[:, at:at + IT * N // 2].bitcast(BF16).rearrange("p (i n) -> p i n", i=IT)
        at += IT * N // 2
        xq = [area.bitcast(BF16).rearrange("p (t c) -> p t c", t=NT)
              for area in (stage[:, 1, 0:NT * HC // 2], scratch[:, at:at + NT * HC // 2])]
        ds_bc = stage[:, 0, :]
        sig, hid = V2[:, :, 0:N], V2[:, :, HC:HC + N]
        iota_i = scratch[:, 3 * C:3 * C + N].bitcast(I32)
        gu_ps = PS[:, 2, :].bitcast(BF16).rearrange("p (k i) -> p k i", k=KT)
        dn_ps = PS[:, 3, :].bitcast(BF16)[:, 0:IT * P].rearrange("p (i o) -> p i o", i=IT)

        WO, GATE, UP, DOWN, RED = (0, 4, 6), (0, 1, 2), (3, 6, 7), (0, 1, 2, 3, 6, 7), ((2, 3), (4, 5))

        def wo_chunk(c):
            if c < RING:
                return [ring[i][:, c, :] for i in range(2)]
            area, at_c = (QT, (c - RING) * C) if c < 7 else (AT, 0)
            return [area[i][:, :, :].rearrange("p k n -> p (k n)")[:, at_c:at_c + C] for i in range(2)]

        def xq_ps(b):
            return PS[:, 4 + b, :].bitcast(BF16)[:, 0:2 * N].rearrange("p (k n) -> p k n", k=2)

        stage_in = [sem(f"stage_in{i}") for i in range(STAGE)]
        w_high = sem("w_high")
        w_low = sem("w_low")
        w_used = sem("w_used")
        x_in = [sem(f"x_in{i}") for i in range(NT)]
        edges_in = sem("edges_in")
        small_in = sem("small_in")
        bc_in = sem("bc_in")
        bo_added = sem("bo_added")
        consts = sem("consts")
        dve_chain = sem("dve_chain")
        act_chain = sem("act_chain")
        var_ready = sem("var_ready")
        root_ready = sem("root_ready")
        y_ready = sem("y_ready")
        t_full = sem("t_full")
        t_high = sem("t_high")
        t_low = sem("t_low")
        proj_high = sem("proj_high")
        proj_low = sem("proj_low")
        acc_free = sem("acc_free")
        keys_made = sem("keys_made")
        keys_out = sem("keys_out")
        key_in = [sem(f"key_in{i}") for i in range(2)]
        key_used = sem("key_used")
        oh_ready = sem("oh_ready")
        oh_used = sem("oh_used")
        diag_ready = sem("diag_ready")
        code_full = sem("code_full")
        ffn_in = [sem(f"ffn_in{i}") for i in range(2)]
        ffn_q = sem("ffn_q")
        ffn_full = sem("ffn_full")
        ffn_evac = sem("ffn_evac")
        s_full = sem("s_full")
        s_seen = sem("s_seen")
        s_free = sem("s_free")
        nb_ready = sem("nb_ready")
        exp_done = sem("exp_done")
        p_ready = sem("p_ready")
        vp_high = sem("vp_high")
        vp_seen = sem("vp_seen")
        vp_low = sem("vp_low")
        o_full = sem("o_full")
        o_high = sem("o_high")
        o_low = sem("o_low")
        soft_in = sem("soft_in")
        ds_turned = sem("ds_turned")
        ds_made = sem("ds_made")
        dsc_out = sem("dsc_out")
        dsbc_in = sem("dsbc_in")
        red_t = sem("red_t")
        red_m = sem("red_m")
        red_b = sem("red_b")
        wo_full = sem("wo_full")
        centred = sem("centred")
        x_scaled = sem("x_scaled")
        t_ready = sem("t_ready")
        xq_ready = sem("xq_ready")
        xqt_full = sem("xqt_full")
        xqt_evac = sem("xqt_evac")
        scales_ready = sem("scales_ready")
        gu_full = sem("gu_full")
        sig_ready = sem("sig_ready")
        h_scale = sem("h_scale")
        ht_ready = sem("ht_ready")
        hq_ready = sem("hq_ready")
        d_full = sem("d_full")
        ds_scaled = sem("ds_scaled")
        d_scaled = sem("d_scaled")
        y_out = [sem(f"y_out{i}") for i in range(2)]
        out_done = sem("out_done")

        class Chain:

            def __init__(self, eng, s):
                self.eng, self.sem, self.n = eng, s, 0

            def link(self, ins):
                ins.then_inc(self.sem, 1)
                self.n = self.n + 1

            def join(self):
                self.eng.wait_ge(self.sem, self.n)

            def step(self, ins):
                self.link(ins)
                self.join()

        block = ctx.enter_context(nc.Block())

        @block.sync
        def _(sp):
            def load(c, slot):
                sp.dma_start(stage[:, slot, :], weights[bass.ds(c, 1), :, :].rearrange("c p n -> p (c n)")
                             ).then_inc(stage_in[slot], 16)

            def load_ffn(i, j):
                slot = j % 2
                sp.wait_ge(ffn_q, 4 * i + (j + 1))
                buf = 2 if i == 0 and slot == 1 else slot
                if j < IT:
                    sp.dma_start(gu_in[buf], w_gate_up[bass.ds(IT * i + j, 1), :, :].rearrange(
                        "s p (b n) -> p (s b) n", b=2)
                                 ).then_inc(ffn_in[slot], 16)
                sp.dma_start(dn_in[buf], w_down[bass.ds(4 * i + j, 1), :, :].rearrange("s p n -> p (s n)")
                             ).then_inc(ffn_in[slot], 16)

            for t in (0, 2):
                sp.dma_start(X[:, t, :], x[t * P:(t + 1) * P, :]).then_inc(x_in[t], 16)
            for c in range(STAGE):
                load(c, c)

            def chunks(first, last):
                with sp.Fori(first // 2, last // 2) as i:
                    for j in range(2):
                        sp.wait_ge(w_low, 2 * i + (j - 1))
                        load(2 * i + j, j)

            chunks(2, 4)
            sp.wait_ge(keys_made, 1)
            sp.dma_start(key_rows, key_row[:, :]).then_inc(keys_out, 16)
            sp.wait_ge(keys_out, 16)

            def keys_and_chunks(first, last):
                with sp.Fori(first, last) as i:
                    for j in range(2):
                        sp.wait_ge(key_used, 2 * i + (j + 1))
                        sp.dma_start(key_bc[:, j, :, :], key_rows[bass.ds((2 * i + j) * EPS, EPS), :].unsqueeze(0)
                                     .to_broadcast([P, EPS, P])).then_inc(key_in[j], 16)
                        sp.wait_ge(w_low, 2 * i + (j + 3))
                        load(2 * i + (j + 4), j)

            keys_and_chunks(0, 2)
            sp.wait_ge(t_full, KT)
            load_ffn(0, 0)
            keys_and_chunks(2, 3)
            load_ffn(0, 1)
            keys_and_chunks(3, 4)
            for s in range(2, 8):
                sp.wait_ge(w_low, s + 9)
                load(s + 10, s % STAGE)
                if s == 5:
                    sp.wait_ge(key_used, 8 + 2)
                load_ffn(s // 4, s % 4)
            chunks(18, 38)
            sp.wait_ge(ds_made, 1)
            sp.dma_start(down_scale_row.rearrange("(s p) -> s p", p=P), ds_row[:, :]).then_inc(dsc_out, 16)
            chunks(38, CHUNKS)
            sp.wait_ge(dsc_out, 16)
            sp.wait_ge(w_low, CHUNKS - 1)
            sp.dma_start(ds_bc, down_scale_row.rearrange("(a n) -> a n", a=1).to_broadcast([P, C])
                         ).then_inc(dsbc_in, 16)
            for m in range(NT):
                for hf in range(2):
                    cs = slice(hf * HC, (hf + 1) * HC)
                    sp.wait_ge(y_out[hf], m + 1)
                    sp.dma_start(out[m * P:(m + 1) * P, cs], X[:, m, cs]).then_inc(out_done, 16)
            sp.wait_ge(out_done, 16 * 2 * NT)

        @block.gpsimd
        def _(pool):
            pool.memset(ident[:, :], 0.0).then_inc(consts, 1)
            pool.memset(wide[:, :], 0.0).then_inc(consts, 1)
            pool.memset(tri[:, :], 1.0).then_inc(consts, 1)
            pool.memset(ones[:, :], 1.0).then_inc(consts, 1)
            for w in range(4):
                ins = pool.memset(kinds[:, w:w + 1], float(w))
            ins.then_inc(consts, 1)
            pool.wait_ge(consts, 5)
            pool.affine_select(out=ident[:, :], in_=ident[:, :], compare_op=ALU.not_equal, fill=1.0,
                               base=0, pattern=[[-1, P]], channel_multiplier=1).then_inc(consts, 1)
            pool.affine_select(out=wide[:, 2 * P:3 * P], in_=wide[:, 2 * P:3 * P], compare_op=ALU.not_equal,
                               fill=1.0, base=0, pattern=[[-1, P]], channel_multiplier=1).then_inc(consts, 1)
            pool.affine_select(out=tri[:, :], in_=tri[:, :], compare_op=ALU.is_ge,
                               fill=0.0, base=-1, pattern=[[1, P]], channel_multiplier=-1).then_inc(consts, 1)
            pool.iota(iota_i, pattern=[[1, N]], base=0, channel_multiplier=0).then_inc(consts, 1)
            pool.iota(code_e[:, :], pattern=[[4, EC]], base=CODE_LOW + 127,
                      channel_multiplier=0).then_inc(consts, 1)

            def low(c, slot):
                pool.wait_ge(w_high, c + 1)
                pool.tensor_tensor(ring[1][:, slot, :], stage[:, slot % STAGE, :],
                                   ring[0][:, slot, :].bitcast(F32), ALU.subtract).then_inc(w_low, 1)

            for c in range(CIV):
                low(c, c % RING)
                if c == 2:
                    pool.wait_ge(bc_in, 16)
                    pool.wait_ge(y_ready, NT)
                if c >= 2:
                    m, hf = (c - 2) // 2, c % 2
                    cs = slice(hf * HC, (hf + 1) * HC)
                    pool.tensor_tensor(X[:, m, cs], X[:, m, cs], bo_bc[:, cs], ALU.add).then_inc(bo_added, 1)
            with pool.Fori(0, 6) as i:
                for j in range(4):
                    low(4 * i + (CIV + j), j)
            for c in range(CPAIR, CPAIR + 4):
                low(c, c % RING)

            def spare_low(c):
                pool.wait_ge(w_high, c + 1)
                high, low_part = wo_chunk(c - CO)
                pool.tensor_tensor(low_part, stage[:, c % STAGE, :], high.bitcast(F32), ALU.subtract).then_inc(w_low, 1)

            def pair_v(u):
                pool.wait_ge(o_full, 2 * u + 1)
                pool.tensor_copy(VP[0][:, :, :], V2[:, :, bass.ds(u * P, P)]).then_inc(vp_high, 1)
                pool.wait_ge(vp_high, u + 1)
                pool.sem_inc(vp_seen, 1)
                pool.tensor_tensor(VP[1][:, :, :], V2[:, :, bass.ds(u * P, P)],
                                   VP[0][:, :, :].bitcast(F32), ALU.subtract).then_inc(vp_low, 1)

            pair_v(0)
            low(36, 0)
            low(37, 1)
            with pool.Fori(0, 3) as i:
                for b in range(2):
                    low(4 * i + (38 + 2 * b), (2 + 2 * b) % RING)
                    low(4 * i + (39 + 2 * b), (3 + 2 * b) % RING)
                    pair_v(2 * i + (b + 1))
            low(50, 2)
            low(51, 3)
            spare_low(52)
            pair_v(7)
            for c in range(53, CHUNKS):
                spare_low(c)
            for t in range(0, 2 * NT, 2):
                pool.wait_ge(d_scaled, t + 1)
                pool.tensor_tensor(X[:, t // 2, 0:HC], X[:, t // 2, 0:HC], V2[:, t // 2, 0:HC], ALU.add
                                   ).then_inc(y_out[0], 1)

        @block.scalar
        def _(act):
            chain = Chain(act, act_chain)
            act.dma_start(X[:, 1, :], x[P:2 * P, :]).then_inc(x_in[1], 16)
            act.dma_start(edge_row[:, :, :], edge_rows).then_inc(edges_in, 16)
            act.dma_start(edges[:, :, :], edge_cols).then_inc(edges_in, 16)
            act.dma_start(bias[:, :], biases).then_inc(small_in, 16)
            act.dma_start(ew[:, 0, :], edge_w.rearrange("(a n) -> a n", a=1).to_broadcast([P, 4])
                          ).then_inc(small_in, 16)
            act.dma_start(clip[:, 0, :], clips.rearrange("(a n) -> a n", a=1).to_broadcast([P, 2])
                          ).then_inc(small_in, 16)
            act.dma_start(bo_bc, bias_o.rearrange("(a n) -> a n", a=1).to_broadcast([P, C])).then_inc(bc_in, 16)
            act.wait_ge(consts, 10)
            chain.step(act.activation(rs[:, 4, :], kinds[:, 0:NT], ACT.Sqrt))

            def high(c2, c, slot):
                act.wait_ge(stage_in[slot % STAGE], 16 * (c2 + 1))
                act.wait_ge(w_used, c + 1)
                act.activation(ring[0][:, slot, :], stage[:, slot % STAGE, :], ACT.Copy).then_inc(w_high, 1)

            def spare_high(c):
                act.wait_ge(stage_in[c % STAGE], 16 * (c // 2 + 1))
                act.wait_ge(w_used, RING + (CO if c == CHUNKS - 1 else CO - 1))
                act.activation(wo_chunk(c - CO)[0], stage[:, c % STAGE, :], ACT.Copy).then_inc(w_high, 1)

            def t_take(tau, bank, dst):
                act.wait_ge(t_full, tau + 1)
                act.activation(dst, PS[:, bank, 0:N], ACT.Copy).then_inc(t_high, 1)

            for m in range(NT):
                act.wait_ge(var_ready, m + 1)
                act.activation(rs[:, 1, m:m + 1], rs[:, 0, m:m + 1], ACT.Sqrt).then_inc(root_ready, 1)
                if m < AHEAD:
                    high(0, m, m)
            for k in range(KT):
                t_take(k, k, XT[0][:, k, :])
            def early(dst, chunk0, bias0):
                with act.Fori(0, 2) as i:
                    for j in range(4):
                        high(2 * i + ((chunk0 + AHEAD + j) // 2), 4 * i + (chunk0 + AHEAD + j), (j + AHEAD) % RING)
                        act.wait_ge(w_used, 4 * i + (RING + chunk0 + j + 1))
                        act.activation(dst[0][:, bass.ds(4 * i + j, 1), :].rearrange("p k n -> p (k n)"),
                                       PS[:, PROJ + j % 2, 0:N], ACT.Identity,
                                       bias=bias[:, bass.ds(4 * i + (bias0 + j), 1)]).then_inc(proj_high, 1)

            act.wait_ge(small_in, 3 * 16)
            early(AT, CV, BIAS_V)

            act.wait_ge(bo_added, 2 * NT)
            with act.Fori(0, 2) as i:
                for j in range(4):
                    high(2 * i + ((CIV + AHEAD + j) // 2), 4 * i + (CIV + AHEAD + j), (j + AHEAD) % RING)
                    if j == 3:
                        act.wait_ge(w_used, 4 * i + (RING + CIV + 4))
                        act.wait_ge(ffn_q, 4 * i + (4 + 2))
                        for m in range(NT):
                            act.activation(V2[:, m, bass.ds(i * HC, HC)], PS[:, INNER_V[m], :], ACT.Copy
                                           ).then_inc(acc_free, 1)
                    act.wait_ge(ffn_full, 4 * i + (j + 1))
                    if j < IT:
                        i0, iw = I_TILES[j]
                        act.activation(guT[:, :, bass.ds(I_F * i + i0, iw)], gu_ps[:, :, 0:iw], ACT.Copy)
                    for t, (_, iw) in enumerate(I_TILES):
                        ins = act.activation(wdT[0:iw, t, bass.ds(4 * P * i + j * P, P)], dn_ps[0:iw, t, :], ACT.Copy)
                    ins.then_inc(ffn_evac, 1)

            chain.step(act.activation(ew[:, 1, :], ew[:, 0, :], ACT.Abs))
            chain.step(act.activation(ew[:, 2, :], ew[:, 1, :], ACT.Exp, scale=-1.0))
            act.activation(ew[:, 3, :], ew[:, 2, :], ACT.Ln, bias=1.0).then_inc(soft_in, 1)
            act.activation(clip[:, 1, :], clip[:, 0, :], ACT.Exp, scale=-1.0).then_inc(soft_in, 1)

            early(QT, CQ, BIAS_Q)
            early(AT, CK, BIAS_K)

            def q_high(t):
                act.wait_ge(w_used, 2 * t + (RING + CPAIR + 1))
                for h, r in enumerate(ROWS):
                    ins = act.activation(QP[h][r, :], PS[r, PROJ, 0:N], ACT.Identity,
                                         bias=bias[r, bass.ds(t + BIAS_IQ, 1)])
                ins.then_inc(proj_high, 1)

            def k_high(t):
                act.wait_ge(w_used, 2 * t + (RING + CPAIR + 2))
                for h, r in enumerate(ROWS):
                    for to in (ROWS[1 - h], r):
                        ins = act.activation(KH[h][to, :], PS[r, PROJ + 1, 0:N], ACT.Identity,
                                             bias=bias[r, bass.ds(t + BIAS_IK, 1)])
                ins.then_inc(proj_high, 1)

            def exps(p, h):
                act.wait_ge(nb_ready, 2 * p + (h + 1))
                for m in range(NT):
                    ins = act.activation(SM[h][:, m, :], SM[h][:, m, :], ACT.Exp, scale=SCALE,
                                         bias=smx[:, 1, h * NT + m:h * NT + m + 1],
                                         accum_out=smx[:, 2, h * NT + m:h * NT + m + 1])
                ins.then_inc(exp_done, 1)

            def o_take(u, h):
                r = slice(h * D, h * D + D)
                act.wait_ge(o_full, 2 * u + (h + 2))
                act.activation(XT[0][r, bass.ds(u, 1), :].rearrange("p k n -> p (k n)"), PS[r, OUT + h, 0:N],
                               ACT.Identity, bias=bias[r, bass.ds(u + BIAS_IV, 1)]).then_inc(o_high, 1)

            def probs_high(u, first, last):
                for n in range(first, last):
                    t_take(6 * u + (8 + n), TPOSE + n % 2, PT[n // NT][0][:, n % NT, :])

            high(17, 34, 2)
            q_high(0)
            high(17, 35, 3)
            k_high(0)
            high(18, 36, 0)
            exps(0, 0)
            q_high(1)
            exps(0, 1)
            probs_high(0, 0, 2)
            high(18, 37, 1)

            def pair(u, half, c, slot):
                probs_high(u, 2, 4)
                k_high(u + 1)
                probs_high(u, 4, 6)
                high(half, c, slot)
                o_take(u, 0)
                high(half, c + 1, slot + 1)
                exps(u + 1, 0)
                q_high(u + 2)
                exps(u + 1, 1)
                probs_high(u + 1, 0, 2)
                o_take(u, 1)

            with act.Fori(0, 3) as i:
                for b in range(2):
                    pair(2 * i + b, 2 * i + (19 + b), 4 * i + (38 + 2 * b), (2 + 2 * b) % RING)
            high(25, 50, 2)
            probs_high(6, 2, 4)
            k_high(7)
            probs_high(6, 4, 6)
            high(25, 51, 3)
            o_take(6, 0)
            spare_high(52)
            exps(7, 0)
            spare_high(53)
            exps(7, 1)
            probs_high(7, 0, 2)
            o_take(6, 1)
            spare_high(54)
            probs_high(7, 2, 6)
            spare_high(55)
            o_take(7, 0)
            o_take(7, 1)
            chain.step(act.activation(rs[:, 4, :], kinds[:, 0:NT], ACT.Sqrt))
            for m in range(NT):
                act.wait_ge(var_ready, NT + m + 1)
                act.activation(rs[:, 1, m:m + 1], rs[:, 0, m:m + 1], ACT.Sqrt).then_inc(root_ready, 1)
                act.activation(V2[:, m, :], X[:, m, :], ACT.Identity, bias=nmean[:, m:m + 1]).then_inc(centred, 1)
            chain.step(act.activation(rs[:, 4, :], kinds[:, 0:NT], ACT.Sigmoid))
            act.wait_ge(centred, NT)
            act.wait_ge(x_scaled, 1)
            for hf in range(2):
                for m in range(NT):
                    half = V2[:, m, hf * HC:(hf + 1) * HC]
                    act.activation(half, half, ACT.Copy, scale=rs[:, 5, m:m + 1]).then_inc(t_ready, 1)
            for k in range(KT // 2):
                act.wait_ge(xqt_full, k + 1)
                act.activation(xqT[:, 2 * k:2 * k + 2, :], xq_ps(k % 2), ACT.Copy).then_inc(xqt_evac, 1)
            act.wait_ge(scales_ready, 1)
            for i, (_, iw) in enumerate(I_TILES):
                act.wait_ge(gu_full, i + 1)
                act.activation(sig[0:iw, i, :], PS[0:iw, GATE[i], 0:N], ACT.Sigmoid,
                               scale=wsc[0:iw, 2, i:i + 1]).then_inc(sig_ready, 1)
            act.wait_ge(h_scale, 1)
            for i, (_, iw) in enumerate(I_TILES):
                act.activation(hid[0:iw, i, :], hid[0:iw, i, :], ACT.Copy,
                               scale=gmx[0:iw, 12:13]).then_inc(ht_ready, 1)
            act.wait_ge(dsbc_in, 16)
            act.activation(ds_bc, ds_bc, ACT.Copy, scale=gmx[:, 10:11]).then_inc(ds_scaled, 1)

        @block.tensor
        def _(pe):
            pe.sem_inc(w_used, RING)
            pe.sem_inc(oh_used, EPS)
            pe.sem_inc(o_full, 1)
            pe.wait_ge(consts, 10)
            for m in range(NT):
                pe.wait_ge(y_ready, m + 1)
                for k in range(KT):
                    ins = pe.transpose(PS[:, k, m * P:(m + 1) * P], V2[:, m, k * P:(k + 1) * P], ident[:, :])
                    if m == NT - 1:
                        ins.then_inc(t_full, 1)

            def passes(outs, lhs, rhs, start, stop):
                for n, (a, b) in enumerate(((0, 0), (0, 1), (1, 0))):
                    ins = pe.matmul(outs, lhs[a], rhs[b], start=start and n == 0, stop=stop and n == 2,
                                    skip_group_check=True)
                return ins

            def begin(c, a):
                pe.wait_ge(w_low, c + 1)
                if a is not None:
                    pe.wait_ge(proj_low, a + 1)

            def part(slot, bank, src, ks, after=None, turned=False):
                w = [ring[i][:, slot, :].rearrange("p (k o) -> p k o", k=KT) for i in range(2)]
                for k in ks:
                    if turned:
                        pe.wait_ge(t_low, k + 3)
                    ins = passes(PS[:, PROJ + bank, 0:N], [w[i][:, k, :] for i in range(2)],
                                 [src[i][:, k, :] for i in range(2)], k == 0, k == KT - 1)
                    if after and k < KT - 1:
                        after(k)
                return ins

            def finish(ins):
                ins.then_inc(w_used, 1)

            def project(c, a, slot, src):
                begin(c, a)
                finish(part(slot, slot % 2, src, range(KT)))

            with pe.Fori(0, 2) as i:
                for j in range(4):
                    begin(4 * i + j, 4 * i + j)
                    pe.wait_ge(t_low, j + 3)
                    finish(part(j, j % 2, XT, range(KT), turned=j == 0))

            def ffn_turn(i, j):
                pe.wait_ge(ffn_q, 4 * i + (j + 3))
                pe.wait_ge(ffn_evac, 4 * i + (j + 1))
                if j < IT:
                    iw = I_TILES[j][1]
                    for k in range(KT):
                        pe.transpose(gu_ps[:, k, 0:iw], gu_q[0:iw, k // 4, k % 4 * P:(k % 4 + 1) * P], wide[0:iw, 2 * P:2 * P + iw])
                for t, (i0, iw) in enumerate(I_TILES):
                    ins = pe.transpose(dn_ps[0:iw, t, :], dn_q[:, i0:i0 + iw], wide[:, 2 * P:3 * P])
                ins.then_inc(ffn_full, 1)

            with pe.Fori(0, 2) as i:
                for j in range(4):
                    pe.wait_ge(w_low, 4 * i + (CIV + j + 1))
                    pe.wait_ge(proj_low, 2 * j + 4)
                    w = [ring[s][:, j, :].rearrange("p (k o) -> p k o", k=2) for s in range(2)]
                    for k2 in range(2):
                        k = 2 * j + k2
                        for m in range(NT):
                            if k == 0:
                                pe.wait_ge(acc_free, NT * i + (m + 1))
                                if m == 2:
                                    pe.wait_ge(proj_low, 7 + 2)
                            ins = passes(PS[:, INNER_V[m], :], [AT[s][:, k, m * P:(m + 1) * P] for s in range(2)],
                                         [w[s][:, k2, :] for s in range(2)], k == 0, k == KT - 1)
                    ins.then_inc(w_used, 1)
                    ffn_turn(i, j)

            pe.wait_ge(diag_ready, 1)
            for s in range(NT):
                if ACC + s == INNER_V[1]:
                    pe.wait_ge(acc_free, 3 * NT - 1)
                pe.matmul(PS[:, ACC + s, 0:N], diag[:, :], wide[:, (2 - s) * P:(5 - s) * P], start=True, stop=False,
                          skip_group_check=True)

            def edge(e, slot):
                pe.wait_ge(oh_ready, e + 1)
                for s in range(NT):
                    ins = pe.matmul(PS[:, ACC + s, 0:N], onehot[:, slot, 0, s * P:(s + 1) * P],
                                    onehot[:, slot, 1, :], start=False, stop=False, skip_group_check=True)
                ins.then_inc(oh_used, 1)

            with pe.Fori(0, 2) as i:
                for j in range(4):
                    first = 2 * sum(ONE_HOT) * i + (sum(ONE_HOT) * (j // 2) + ONE_HOT[0] * (j % 2))
                    begin(4 * i + (CQ + j), 4 * i + (8 + j))
                    if j == 0:
                        pe.wait_ge(acc_free, 3 * NT)
                    finish(part(j, j % 2, XT, range(KT), lambda k: edge(first + k, k) if k < ONE_HOT[j % 2] else None))
            for s in range(NT):
                ins = pe.matmul(PS[:, ACC + s, 0:N], wide[:, 0:P], wide[:, 0:N], start=False, stop=True,
                                skip_group_check=True)
            ins.then_inc(code_full, 1)

            with pe.Fori(0, 2) as i:
                for j in range(4):
                    project(4 * i + (CK + j), 4 * i + (16 + j), j, XT)

            pe.wait_ge(ffn_evac, 8 + 1)
            pe.transpose(PS[0:KT, TPOSE, 0:P], dsc[:, 1, :], ident[:, :]).then_inc(ds_turned, 1)

            def score(p, m):
                for h in range(2):
                    pe.wait_ge(s_free, 6 * p + (2 * m + h + 1))
                    for k in (KH, KL):
                        ins = pe.matmul(PS[:, SCORE + h, 0:N], QP[h][:, m * P:(m + 1) * P], k[h][:, :],
                                        start=k is KH, stop=k is KL)
                    ins.then_inc(s_full, 1)

            def turn_probs(u, h, m):
                if m == 0:
                    pe.wait_ge(p_ready, 2 * u + (h + 1))
                pe.wait_ge(t_low, 6 * u + (8 + 3 * h + m + 1))
                for n in range(NT):
                    ins = pe.transpose(PS[:, TPOSE + (h * NT + m) % 2, n * P:(n + 1) * P],
                                       SM[h][:, n, m * P:(m + 1) * P], ident[:, :])
                ins.then_inc(t_full, 1)

            def weigh(u, h):
                pe.wait_ge(vp_low, u + 1)
                pe.wait_ge(t_low, 6 * u + (8 + 3 * h + 3 + 2))
                pe.wait_ge(o_low, 2 * u + (h + 1))
                for m in range(NT):
                    ins = passes(PS[:, OUT + h, 0:N], [VP[s][:, m, :] for s in range(2)],
                                 [PT[h][s][:, m, :] for s in range(2)], m == 0, m == NT - 1)
                ins.then_inc(o_full, 1)

            project(32, 24, 0, QT)
            project(33, 25, 1, AT)
            begin(34, 26)
            part(2, 0, QT, range(0, 6))
            pe.wait_ge(proj_low, 26 + 2)
            score(0, 0)
            part(2, 0, QT, range(6, 7))
            score(0, 1)
            finish(part(2, 0, QT, range(7, 8)))
            score(0, 2)
            project(35, 27, 3, AT)
            turn_probs(0, 0, 0)
            turn_probs(0, 0, 1)

            def pair(u, c0, slot0):
                a0 = 2 * u + 28
                begin(c0, a0)
                part(slot0, 0, QT, range(0, 4))
                turn_probs(u, 0, 2)
                turn_probs(u, 1, 0)
                part(slot0, 0, QT, range(4, 6))
                turn_probs(u, 1, 1)
                turn_probs(u, 1, 2)
                finish(part(slot0, 0, QT, range(6, 8)))
                weigh(u, 0)
                pe.wait_ge(proj_low, a0 + 2)
                score(u + 1, 0)
                begin(c0 + 1, a0 + 1)
                part(slot0 + 1, 1, AT, range(0, 1))
                score(u + 1, 1)
                part(slot0 + 1, 1, AT, range(1, 2))
                score(u + 1, 2)
                part(slot0 + 1, 1, AT, range(2, 6))
                weigh(u, 1)
                finish(part(slot0 + 1, 1, AT, range(6, 8)))
                turn_probs(u + 1, 0, 0)
                turn_probs(u + 1, 0, 1)

            with pe.Fori(0, 3) as i:
                for b in range(2):
                    pair(2 * i + b, 4 * i + (36 + 2 * b), 2 * b)

            def output(m, hf, j):
                w = [chunk[:, :].rearrange("p (k o) -> p k o", k=2) for chunk in wo_chunk(4 * hf + j)]
                if m == 0:
                    pe.wait_ge(w_low, CO + 4 * hf + j + 1)
                    pe.wait_ge(o_low, 4 * (j + 1) + 2)
                for k2 in range(2):
                    k = 2 * j + k2
                    ins = passes(PS[:, WO[m] + hf, :], [XT[i][:, k, m * P:(m + 1) * P] for i in range(2)],
                                 [w[i][:, k2, :] for i in range(2)], k == 0, k == KT - 1)
                if j == 3:
                    ins.then_inc(wo_full, 1)

            pe.wait_ge(proj_low, 39 + 2)
            output(0, 0, 0)
            turn_probs(6, 0, 2)
            turn_probs(6, 1, 0)
            output(0, 0, 1)
            turn_probs(6, 1, 1)
            turn_probs(6, 1, 2)
            weigh(6, 0)
            pe.wait_ge(proj_low, 40 + 2)
            score(7, 0)
            score(7, 1)
            score(7, 2)
            weigh(6, 1)
            output(0, 0, 2)
            output(0, 1, 0)
            turn_probs(7, 0, 0)
            turn_probs(7, 0, 1)
            output(1, 0, 0)
            turn_probs(7, 0, 2)
            turn_probs(7, 1, 0)
            output(0, 1, 1)
            turn_probs(7, 1, 1)
            turn_probs(7, 1, 2)
            weigh(7, 0)
            output(1, 0, 1)
            weigh(7, 1)
            output(0, 1, 2)

            output(0, 0, 3)
            output(0, 1, 3)
            for m in range(1, NT):
                for hf in range(2):
                    for j in range(2 if (m, hf) == (1, 0) else 0, 4):
                        output(m, hf, j)

            def keep_clock(n):
                for _ in range(n):
                    pe.matmul(PS[:, 0, 0:N], wide[:, 0:P], wide[:, 0:N], start=True, stop=True)

            def reduce_max(n):
                row, all_rows = RED[n]
                for i in range(3):
                    pe.wait_ge(red_t, 3 * n + i + 1)
                    ins = pe.transpose(PS[0:1, row, i * P:(i + 1) * P], gmx[:, 4 * n + i:4 * n + i + 1], ident[:, :])
                    if n == 1 and i < 2:
                        keep_clock(2)
                ins.then_inc(red_b, 1)
                pe.wait_ge(red_m, n + 1)
                pe.matmul(PS[:, all_rows, 0:1], ones[:, :], gmx[0:1, 8:9], start=True, stop=True).then_inc(red_b, 1)

            reduce_max(0)
            keep_clock(14)

            def turn_ints(k):
                pe.wait_ge(xq_ready, k // 2 * NT + NT)
                if k >= 2:
                    pe.wait_ge(xqt_evac, k - 1)
                for k2 in range(2):
                    for m in range(NT):
                        cs = slice((k % 2 * 2 + k2) * P, (k % 2 * 2 + k2 + 1) * P)
                        ins = pe.transpose(xq_ps(k % 2)[:, k2, m * P:(m + 1) * P], xq[k // 2][:, m, cs],
                                           wide[:, 2 * P:3 * P])
                ins.then_inc(xqt_full, 1)

            turn_ints(0)
            turn_ints(1)
            for hf in range(2):
                for g in range(2):
                    if (hf, g) == (0, 1):
                        turn_ints(2)
                        turn_ints(3)
                    for i, (i0, iw) in enumerate(I_TILES):
                        for k in range(4 * hf, 4 * hf + 4):
                            if (g, i, k % 2) == (0, 0, 0):
                                pe.wait_ge(xqt_evac, k // 2 + 1)
                            ins = pe.matmul(PS[0:iw, (GATE, UP)[g][i], 0:N], guT[:, k, g * I_F + i0:g * I_F + i0 + iw],
                                            xqT[:, k, :], start=(k == 0), stop=(k == KT - 1), skip_group_check=True)
                        if hf == 1:
                            ins.then_inc(gu_full, 1)
            reduce_max(1)
            keep_clock(8)
            for t in range(2 * NT):
                m, hf = t // 2, t % 2
                for i, (_, iw) in enumerate(I_TILES):
                    if t == 0:
                        pe.wait_ge(hq_ready, i + 1)
                    ins = pe.matmul(PS[:, DOWN[t], :], hq[0:iw, i, m * P:(m + 1) * P],
                                    wdT[0:iw, i, hf * HC:(hf + 1) * HC], start=(i == 0), stop=(i == IT - 1))
                ins.then_inc(d_full, 1)

        @block.vector
        def _(dve):
            chain = Chain(dve, dve_chain)
            dve.sem_inc(t_low, 2)
            dve.sem_inc(proj_low, 2)
            dve.sem_inc(acc_free, NT)
            dve.sem_inc(key_used, 2)
            dve.sem_inc(ffn_q, 2)
            dve.sem_inc(ffn_evac, 1)
            dve.sem_inc(s_free, 2)
            dve.sem_inc(o_low, 2)
            def moments(m):
                for g in range(2):
                    chain.link(dve.bn_stats(stats[:, m, g, :], X[:, m, g * HC:(g + 1) * HC]))
                chain.join()
                chain.step(dve.bn_aggr(mv[:, m, :], stats[:, m, :, :].rearrange("p a b -> p (a b)")))
                dve.tensor_scalar(rs[:, 0, m:m + 1], mv[:, m, 1:2], LN_EPS, None, ALU.add).then_inc(var_ready, 1)

            def norm(n, m):
                v, root, inv, two = (rs[:, c, m:m + 1] for c in range(4))
                dve.wait_ge(root_ready, NT * n + m + 1)
                chain.step(dve.reciprocal(inv, root))
                chain.step(dve.scalar_tensor_tensor(two, inv, v, root, ALU.mult, ALU.add))
                chain.step(dve.tensor_scalar(two, two, 0.5, None, ALU.mult))
                chain.step(dve.reciprocal(inv, two))
                dve.tensor_scalar(V2[:, m, :], X[:, m, :], mv[:, m, 0:1], inv,
                                  ALU.subtract, ALU.mult).then_inc(y_ready, 1)

            for m in range(NT):
                dve.wait_ge(x_in[m], 16)
                moments(m)
                if m:
                    norm(0, m - 1)
            norm(0, NT - 1)
            dve.wait_ge(edges_in, 2 * 16)
            dve.scalar_tensor_tensor(key_row[:, :], edge_row[:, 0, :], float(N), edge_row[:, 1, :],
                                     ALU.mult, ALU.add).then_inc(keys_made, 1)

            def t_rest(tau, bank, high, low):
                dve.wait_ge(t_high, tau + 1)
                dve.tensor_tensor(low, PS[:, bank, 0:N], high.bitcast(F32), ALU.subtract).then_inc(t_low, 1)

            for k in range(KT):
                t_rest(k, k, XT[0][:, k, :], XT[1][:, k, :])
            SRC, DST, KEY, TYP, NEG, VAL = range(6)
            chain.link(dve.tensor_copy(ecol[:, SRC, :], edges[:, 0, :]))
            chain.link(dve.tensor_copy(ecol[:, DST, :], edges[:, 1, :]))
            chain.step(dve.tensor_scalar(ecol[:, TYP, :], edges[:, 2, :], 4.0, -1.0, ALU.min, ALU.add))
            chain.link(dve.scalar_tensor_tensor(ecol[:, KEY, :], ecol[:, SRC, :], float(N), ecol[:, DST, :],
                                                ALU.mult, ALU.add))
            chain.step(dve.tensor_scalar(ecol[:, NEG, :], ecol[:, TYP, :], 0.0, 4.0, ALU.is_lt, ALU.mult))
            chain.step(dve.tensor_tensor(ecol[:, TYP, :], ecol[:, TYP, :], ecol[:, NEG, :], ALU.add))
            chain.step(dve.tensor_scalar(ecol[:, TYP, :], ecol[:, TYP, :], 0.25, 1.0, ALU.mult, ALU.add))
            dve.wait_ge(consts, 10)
            chain.step(dve.tensor_scalar(code_e[:, :], code_e[:, :], 23, None, ALU.logical_shift_left))
            chain.link(dve.tensor_tensor(ecol[:, VAL, :], ecol[:, TYP, :], code_e[:, :].bitcast(F32), ALU.mult))
            chain.link(dve.tensor_copy(iota[:, :], iota_i))
            chain.link(dve.memset(gmx[:, 4:4 + IT], 0.0))
            dve.tensor_scalar(diag[:, :], ident[:, :], 1.75 * 2.0 ** (CODE_LOW - 4), None,
                              ALU.mult).then_inc(diag_ready, 1)

            for h in range(2):
                chain.link(dve.memset(KL[h][ROWS[1 - h], :].bitcast(F32), 0.0))

            def tile_low(a, k, b, dst, col):
                dve.wait_ge(proj_high, a + 1)
                at_k = [dst[s][:, bass.ds(k, 1), :].rearrange("p k n -> p (k n)") for s in range(2)]
                dve.scalar_tensor_tensor(at_k[1], PS[:, PROJ + b, 0:N], bias[:, bass.ds(col, 1)],
                                         at_k[0].bitcast(F32), ALU.add, ALU.subtract).then_inc(proj_low, 1)

            dve.wait_ge(small_in, 3 * 16)
            def to_ints(both, turned):
                for src, _, sc, col in both:
                    chain.link(dve.tensor_reduce(sc[:, 0, col], src, AXES[len(src.shape) - 2], ALU.max, apply_absolute_value=True))
                chain.join()
                for _, _, sc, col in both:
                    chain.link(dve.tensor_scalar(sc[:, 1, col], sc[:, 0, col], 1.0 / QMAX, None, ALU.mult))
                chain.join()
                for _, _, sc, col in both:
                    chain.link(dve.reciprocal(sc[:, 2, col], sc[:, 1, col]))
                chain.join()
                for src, _, sc, col in both:
                    chain.link(dve.tensor_scalar(src, src, sc[:, 2, col], MAGIC, ALU.mult, ALU.add))
                chain.join()
                dve.wait_ge(ffn_evac, turned)
                for src, q, _, _ in both:
                    ins = dve.tensor_scalar(q, src, MAGIC, None, ALU.subtract)
                ins.then_inc(ffn_q, 1)

            def later_edge(s, b, n):
                dve.wait_ge(key_in[b], n)
                cols = bass.ds(s * EPS, EPS) if not isinstance(s, int) else slice(s * EPS, (s + 1) * EPS)
                dve.wait_ge(key_used, s + 2)
                chain.step(dve.tensor_tensor(same[:, :, :], key_bc[:, b, :, :],
                                             ecol[:, KEY, cols].unsqueeze(2).to_broadcast([P, EPS, P]),
                                             ALU.is_equal))
                chain.step(dve.tensor_tensor(same[:, :, :], same[:, :, :],
                                             tri[:, :].unsqueeze(1).to_broadcast([P, EPS, P]), ALU.mult))
                dve.tensor_reduce(dup[:, cols], same[:, :, :], X_AXIS, ALU.max).then_inc(key_used, 1)

            def ffn_step(i, j):
                dve.wait_ge(ffn_in[j % 2], [64 * i + 32, 48 * i + 32, 64 * i + 64, 48 * i + 48][j])
                buf = 2 if i == 0 and j % 2 == 1 else j % 2
                gu = [(gu_in[buf], gu_q, wsc, bass.ds(IT * i + j, 1))] if j < IT else []
                to_ints(gu + [(dn_in[buf], dn_q, dsc, bass.ds(4 * i + j, 1))], 4 * i + (j + 1))

            base = chain.n
            with dve.Fori(0, 3) as i:
                for b in range(2):
                    chain.n = 4 * i + (base + 2 * b)
                    tile_low(2 * i + b, 2 * i + b, b, AT, 2 * i + (BIAS_V + b))
                    later_edge(2 * i + b, b, 16 * i + 16)
            chain.n = base + 12
            tile_low(6, 6, 0, AT, BIAS_V + 6)
            ffn_step(0, 0)
            tile_low(7, 7, 1, AT, BIAS_V + 7)
            ffn_step(0, 1)
            later_edge(6, 0, 4 * 16)
            ffn_step(0, 2)
            later_edge(7, 1, 4 * 16)
            dve.wait_ge(key_used, 8 + 2)
            chain.step(dve.tensor_scalar(dup[:, :], dup[:, :], -1.0, 1.0, ALU.mult, ALU.add))
            chain.step(dve.tensor_tensor(ecol[:, VAL, :], ecol[:, VAL, :], dup[:, :], ALU.mult))

            for s in range(3, 8):
                ffn_step(s // 4, s % 4)


            dve.wait_ge(ffn_full, 8)

            def one_hot(first, before, n):
                for s in range(n):
                    e = first + s
                    dve.wait_ge(oh_used, before + (min(s, ONE_HOT[1] - 1) + 1 + EPS))
                    dve.tensor_scalar(onehot[:, s, 0, :], iota[:, :], ecol[:, SRC, bass.ds(e, 1)],
                                      ecol[:, VAL, bass.ds(e, 1)], ALU.is_equal, ALU.mult)
                    dve.tensor_scalar(onehot[:, s, 1, :], iota[:, :], ecol[:, DST, bass.ds(e, 1)],
                                      None, ALU.is_equal).then_inc(oh_ready, 1)

            def q_tile(s, b):
                tile_low(s + 8, s, b, QT, s + BIAS_Q)

            ROUND = sum(ONE_HOT)
            one_hot(0, -EPS, ONE_HOT[0])
            with dve.Fori(0, 3) as i:
                one_hot(ROUND * i + ONE_HOT[0], ROUND * i, ONE_HOT[1])
                q_tile(2 * i, 0)
                one_hot(ROUND * i + ROUND, ROUND * i + ONE_HOT[0], ONE_HOT[0])
                q_tile(2 * i + 1, 1)
            one_hot(3 * ROUND + ONE_HOT[0], 3 * ROUND, ONE_HOT[1])
            q_tile(6, 0)
            q_tile(7, 1)
            dve.wait_ge(soft_in, 2)
            chain.step(dve.scalar_tensor_tensor(ew[:, 4, :], ew[:, 0, :], 0.0, ew[:, 3, :], ALU.max, ALU.add))
            chain.step(dve.tensor_scalar(ew[:, 5, :], ew[:, 4, :], 1.0 / SCALE, None, ALU.mult))
            chain.step(dve.tensor_scalar(clip[:, 2, :], clip[:, 1, :], 1.0, None, ALU.add))
            chain.step(dve.reciprocal(clip[:, 3, :], clip[:, 2, :]))
            chain.step(dve.tensor_scalar(clip[:, 2, :], clip[:, 3, :], 1.0 / QMAX, None, ALU.mult))
            code = PS[:, ACC:ACC + NT, 0:N]
            dve.wait_ge(code_full, 1)
            kind = SM[0].bitcast(I32)
            chain.step(dve.tensor_scalar(kind, code.bitcast(I32), 21, 3, ALU.logical_shift_right, ALU.bitwise_and))
            chain.step(dve.tensor_scalar(mask, code, 0.0, NO_EDGE, ALU.is_equal, ALU.mult))
            base = chain.n
            with dve.Fori(0, 4) as w:
                chain.n = 2 * w + base
                tile_low(2 * w + 16, 2 * w, 0, AT, 2 * w + BIAS_K)
                chain.step(dve.tensor_scalar(SM[1], kind, kinds[:, bass.ds(w, 1)], ew[:, 5, bass.ds(w, 1)],
                                             ALU.is_equal, ALU.mult))
                tile_low(2 * w + 17, 2 * w + 1, 1, AT, 2 * w + (BIAS_K + 1))
                chain.step(dve.tensor_tensor(mask, mask, SM[1], ALU.add))
            chain.n = base + 8

            dve.wait_ge(ds_turned, 1)
            dve.tensor_copy(ds_row[:, :], PS[0:KT, TPOSE, 0:P]).then_inc(ds_made, 1)

            def q_low(t):
                dve.wait_ge(proj_high, 2 * t + 25)
                for h, r in enumerate(ROWS):
                    ins = dve.scalar_tensor_tensor(QP[h][ROWS[1 - h], :], PS[r, PROJ, 0:N],
                                                   bias[r, bass.ds(t + BIAS_IQ, 1)],
                                                   QP[h][r, :].bitcast(F32), ALU.add, ALU.subtract)
                ins.then_inc(proj_low, 1)

            def k_low(t):
                dve.wait_ge(proj_high, 2 * t + 26)
                for h, r in enumerate(ROWS):
                    ins = dve.scalar_tensor_tensor(KL[h][r, :], PS[r, PROJ + 1, 0:N], bias[r, bass.ds(t + BIAS_IK, 1)],
                                                   KH[h][r, :].bitcast(F32), ALU.add, ALU.subtract)
                ins.then_inc(proj_low, 1)

            def masked(p, m):
                for h in range(2):
                    dve.wait_ge(s_full, 6 * p + (2 * m + h + 1))
                    dve.sem_inc(s_seen, 1)
                    dve.tensor_tensor_reduce(SM[h][:, m, :], PS[:, SCORE + h, 0:N], mask[:, m, :], 1.0, -3e38,
                                             ALU.add, ALU.max, smx[:, 0, h * NT + m:h * NT + m + 1]
                                             ).then_inc(s_free, 1)

            def negate(p):
                dve.wait_ge(s_free, 6 * p + (6 + 2))
                for h in range(2):
                    hs = slice(h * NT, (h + 1) * NT)
                    dve.tensor_scalar(smx[:, 1, hs], smx[:, 0, hs], -SCALE, None, ALU.mult).then_inc(nb_ready, 1)

            def normalise(p, h):
                hs = slice(h * NT, (h + 1) * NT)
                dve.wait_ge(exp_done, 2 * p + (h + 1))
                chain.step(dve.reciprocal(smx[:, 3, hs], smx[:, 2, hs]))
                for m in range(NT):
                    ins = dve.tensor_scalar(SM[h][:, m, :], SM[h][:, m, :], smx[:, 3, h * NT + m:h * NT + m + 1],
                                            None, ALU.mult)
                ins.then_inc(p_ready, 1)

            def o_rest(u, h):
                r = slice(h * D, h * D + D)
                at_u = [XT[s][r, bass.ds(u, 1), :].rearrange("p k n -> p (k n)") for s in range(2)]
                dve.wait_ge(o_high, 2 * u + (h + 1))
                dve.scalar_tensor_tensor(at_u[1], PS[r, OUT + h, 0:N], bias[r, bass.ds(u + BIAS_IV, 1)],
                                         at_u[0].bitcast(F32), ALU.add, ALU.subtract).then_inc(o_low, 1)

            q_low(0)
            k_low(0)
            masked(0, 0)
            masked(0, 1)
            masked(0, 2)
            negate(0)
            normalise(0, 0)
            q_low(1)
            normalise(0, 1)

            def probs_low(u, first, last):
                for n in range(first, last):
                    t_rest(6 * u + (8 + n), TPOSE + n % 2, PT[n // NT][0][:, n % NT, :], PT[n // NT][1][:, n % NT, :])

            probs_low(0, 0, 2)

            def pair(u, proj=True):
                probs_low(u, 2, 4)
                k_low(u + 1)
                probs_low(u, 4, 6)
                masked(u + 1, 0)
                masked(u + 1, 1)
                masked(u + 1, 2)
                negate(u + 1)
                o_rest(u, 0)
                normalise(u + 1, 0)
                if proj:
                    q_low(u + 2)
                normalise(u + 1, 1)
                probs_low(u + 1, 0, 2)
                o_rest(u, 1)

            base = chain.n
            with dve.Fori(0, 3) as i:
                for b in range(2):
                    chain.n = 4 * i + (base + 2 * b)
                    pair(2 * i + b)
            chain.n = base + 12
            pair(6, False)
            probs_low(7, 2, 6)
            o_rest(7, 0)
            o_rest(7, 1)

            def greatest(n):
                row, all_rows = RED[n]
                dve.wait_ge(red_b, 2 * n + 1)
                dve.tensor_reduce(gmx[0:1, 8:9], PS[0:1, row, 0:3 * P], X_AXIS, ALU.max).then_inc(red_m, 1)
                dve.wait_ge(red_b, 2 * n + 2)
                chain.step(dve.tensor_tensor(gmx[:, 9 + n:10 + n], PS[:, all_rows, 0:1], clip[:, 2, n:n + 1], ALU.mult))

            most, least, over, under = (smx[:, c, :] for c in range(4))
            for m in range(NT):
                mean, inv = mv[:, m, 0:1], rs[:, 2, m:m + 1]
                for hf in range(2):
                    t = 2 * m + hf
                    cs = slice(hf * HC, (hf + 1) * HC)
                    dve.wait_ge(wo_full, t + 1)
                    dve.sem_inc(s_seen, 1)
                    chain.step(dve.tensor_tensor_reduce(X[:, m, cs], PS[:, WO[m] + hf, :], X[:, m, cs], 1.0, -3e38,
                                                        ALU.add, ALU.max, most[:, t:t + 1]))
                    chain.link(dve.bn_stats(stats[:, m, hf, :], X[:, m, cs]))
                    if t < 2 * NT - 1:
                        chain.link(dve.tensor_reduce(least[:, t:t + 1], X[:, m, cs], X_AXIS, ALU.min))
                chain.join()
                chain.step(dve.bn_aggr(mv[:, m, :], stats[:, m, :, :].rearrange("p a b -> p (a b)")))
                dve.tensor_scalar(nmean[:, m:m + 1], mean, -1.0, None, ALU.mult)
                dve.tensor_scalar(rs[:, 0, m:m + 1], mv[:, m, 1:2], LN_EPS, None, ALU.add).then_inc(var_ready, 1)
                if m == NT - 1:
                    chain.step(dve.tensor_reduce(least[:, t:t + 1], X[:, m, cs], X_AXIS, ALU.min))
                t = 2 * m
                chain.link(dve.tensor_scalar(over[:, m:m + 1], most[:, t:t + 1], most[:, t + 1:t + 2], mean,
                                             ALU.max, ALU.subtract))
                chain.link(dve.tensor_scalar(under[:, m:m + 1], least[:, t:t + 1], least[:, t + 1:t + 2], mean,
                                             ALU.min, ALU.subtract))
                dve.wait_ge(root_ready, NT + m + 1)
                chain.step(dve.reciprocal(inv, rs[:, 1, m:m + 1]))
                chain.link(dve.scalar_tensor_tensor(over[:, m:m + 1], under[:, m:m + 1], -1.0, over[:, m:m + 1],
                                                    ALU.mult, ALU.max))
                chain.step(dve.scalar_tensor_tensor(rs[:, 3, m:m + 1], inv, rs[:, 0, m:m + 1], rs[:, 1, m:m + 1],
                                                    ALU.mult, ALU.add))
                chain.step(dve.reciprocal(inv, rs[:, 3, m:m + 1]))
                dve.tensor_tensor(gmx[:, m:m + 1], over[:, m:m + 1], inv, ALU.mult).then_inc(red_t, 1)

            greatest(0)
            chain.step(dve.reciprocal(gmx[:, 11:12], gmx[:, 9:10]))
            dve.tensor_scalar(rs[:, 5, :], rs[:, 2, :], gmx[:, 11:12], None, ALU.mult).then_inc(x_scaled, 1)
            dve.tensor_scalar(wsc[:, 2, :], wsc[:, 1, :], gmx[:, 9:10], 2.0, ALU.mult, ALU.mult).then_inc(scales_ready, 1)

            def round_off(src, dst):
                chain.step(dve.tensor_scalar(src, src, QMAX, -QMAX - 1.0, ALU.min, ALU.max))
                return dve.tensor_scalar(dst, src, MAGIC, MAGIC, ALU.add, ALU.subtract)

            for hf in range(2):
                for m in range(NT):
                    dve.wait_ge(t_ready, NT * hf + m + 1)
                    round_off(V2[:, m, hf * HC:(hf + 1) * HC], xq[hf][:, m, :]).then_inc(xq_ready, 1)
            for i, (_, iw) in enumerate(I_TILES):
                sg, ht = sig[0:iw, i, :], hid[0:iw, i, :]
                dve.wait_ge(sig_ready, i + 1)
                chain.link(dve.scalar_tensor_tensor(ht, PS[0:iw, GATE[i], 0:N], wsc[0:iw, 2, i:i + 1], sg,
                                                    ALU.mult, ALU.mult))
            chain.join()
            for i, (_, iw) in enumerate(I_TILES):
                ht = hid[0:iw, i, :]
                dve.wait_ge(gu_full, IT + i + 1)
                chain.step(dve.scalar_tensor_tensor(ht, PS[0:iw, UP[i], 0:N], wsc[0:iw, 2, IT + i:IT + i + 1], ht,
                                                    ALU.mult, ALU.mult))
                dve.tensor_reduce(gmx[0:iw, 4 + i:5 + i], ht, X_AXIS, ALU.max, apply_absolute_value=True
                                  ).then_inc(red_t, 1)
            greatest(1)
            dve.reciprocal(gmx[:, 12:13], gmx[:, 10:11]).then_inc(h_scale, 1)
            for i, (_, iw) in enumerate(I_TILES):
                dve.wait_ge(ht_ready, i + 1)
                round_off(hid[0:iw, i, :], hq[0:iw, i, :]).then_inc(hq_ready, 1)
            dve.wait_ge(hq_ready, IT)
            dve.wait_ge(ds_scaled, 1)
            for t in range(2 * NT):
                m, cs = t // 2, slice(t % 2 * HC, (t % 2 + 1) * HC)
                dve.wait_ge(d_full, t + 1)
                dve.tensor_tensor(V2[:, m, cs], PS[:, DOWN[t], :], ds_bc[:, cs], ALU.mult).then_inc(d_scaled, 1)
                if t % 2:
                    dve.wait_ge(d_scaled, t + 1)
                    dve.tensor_tensor(X[:, m, cs], X[:, m, cs], V2[:, m, cs], ALU.add).then_inc(y_out[1], 1)


NAMES = ["x", "weights", "biases", "bias_o", "edge_cols", "edge_rows", "edge_w", "clips",
         "w_gate_up", "w_down"]


def layout(x, src, dst, edge_type_5, L0_gnn_edge_type_weights, L0_gnn_wq, L0_gnn_bq, L0_gnn_wk, L0_gnn_bk,
           L0_gnn_wv, L0_gnn_bv, L0_gnn_wiq, L0_gnn_biq, L0_gnn_wik, L0_gnn_bik, L0_gnn_wiv, L0_gnn_biv,
           L0_gnn_wo, L0_gnn_bo, L0_ffn_clip_x, L0_ffn_clip_down, L0_ffn_w_gate, L0_ffn_w_up, L0_ffn_w_down):
    import numpy as np

    def tiles(w):
        return np.asarray(w).reshape(KT, P, KT, P).transpose(0, 3, 2, 1).reshape(KT, P, C)

    def halves(w):
        return np.asarray(w).reshape(2, HC, 4, 2, P).transpose(0, 2, 4, 3, 1).reshape(8, P, C)

    pairs = np.stack([tiles(L0_gnn_wiq), tiles(L0_gnn_wik)], axis=1).reshape(16, P, C)
    weights = np.concatenate([tiles(L0_gnn_wv), halves(L0_gnn_wiv), tiles(L0_gnn_wq), tiles(L0_gnn_wk), pairs,
                              halves(L0_gnn_wo)])
    biases = np.concatenate([np.asarray(b).reshape(KT, P) for b in
                             (L0_gnn_bv, L0_gnn_bq, L0_gnn_bk, L0_gnn_biq, L0_gnn_bik, L0_gnn_biv)]).T
    ones = np.ones((IT * P - I_F, C), np.float32)
    edge = [np.concatenate([np.asarray(a, np.int32), np.full(EC * P - E, f, np.int32)]).reshape(EC, P)
            for a, f in ((src, -1), (dst, -1), (edge_type_5, 1))]
    return {
        "x": np.asarray(x), "weights": weights, "biases": np.ascontiguousarray(biases),
        "bias_o": np.asarray(L0_gnn_bo),
        "edge_cols": np.ascontiguousarray(np.stack(edge).transpose(2, 0, 1)),
        "edge_rows": np.ascontiguousarray(np.stack(edge[:2]).transpose(1, 0, 2)),
        "edge_w": np.asarray(L0_gnn_edge_type_weights),
        "clips": np.concatenate([np.asarray(L0_ffn_clip_x), np.asarray(L0_ffn_clip_down)]),
        "w_gate_up": np.concatenate([np.asarray(L0_ffn_w_gate), ones, np.asarray(L0_ffn_w_up), ones]
                                    ).reshape(2 * IT, P, C),
        "w_down": np.asarray(L0_ffn_w_down).reshape(KT, P, I_F),
    }


def kernel(**inputs):
    import numpy as np
    import concourse.bacc as bacc
    from concourse.bass_utils import run_bass_kernel_spmd

    nc = bacc.Bacc("TRN2", target_bir_lowering=False, num_devices=1)
    arrays = {f"in_{k}": np.ascontiguousarray(v) for k, v in layout(**inputs).items()}
    args = [nc.dram_tensor(f"in_{n}", arrays[f"in_{n}"].shape, mybir.dt.from_np(arrays[f"in_{n}"].dtype),
                           kind="ExternalInput").ap() for n in NAMES]
    key_rows = nc.dram_tensor("key_rows", (EC, P), F32, kind="Internal").ap()
    down_scale_row = nc.dram_tensor("down_scale_row", (C,), F32, kind="Internal").ap()
    out = nc.dram_tensor("out", (N, C), F32, kind="ExternalOutput").ap()
    gnn_ffn(nc, *args, key_rows, down_scale_row, out)
    result = run_bass_kernel_spmd(nc, [arrays], core_ids=[0])
    return result.results[0]["out"]
```
